# Optimizing a Trainium2 kernel written in Bass

```python
import numpy as np
import jax
import jax.numpy as jnp

def _softmax(x, axis=-1):
    return jax.nn.softmax(x, axis=axis)

def _gelu(x):
    return jax.nn.gelu(x, approximate=True)

def _silu(x):
    return jax.nn.silu(x)

def _sigmoid(x):
    return jax.nn.sigmoid(x)

def _layernorm(x, axis=-1, eps=1e-05):
    m = jnp.mean(x, axis=axis, keepdims=True)
    v = jnp.var(x, axis=axis, keepdims=True)
    return (x - m) / jnp.sqrt(v + eps)

def _scatter_add(tgt, idx, src, axis=0):
    return tgt.at[idx].add(src)

def _segment_sum(src, seg, n):
    return jax.ops.segment_sum(src, seg, n)
kernel_name = 'mk_gnn_resnorm_d1_gnn_r64_75a801'

def setup_inputs(seed: int=0):
    np.random.seed(seed)
    _w = jnp.asarray

    def _rec_inputs():
        import jax
        import jax.numpy as jnp
        _gk = jax.random.key(seed)
        x = -0.000202 + 1 * jax.random.normal(jax.random.fold_in(_gk, 1), (100000, 128), jnp.float32)
        _s = jax.random.randint(jax.random.fold_in(_gk, 2), (12500,), 0, 100000, jnp.int32)
        _d = jax.random.randint(jax.random.fold_in(_gk, 3), (12500,), 0, 100000, jnp.int32)
        _loop = jnp.arange(100000, dtype=jnp.int32)
        src = jnp.concatenate([_s, _d, _loop])
        dst = jnp.concatenate([_d, _s, _loop])
        _o = jnp.argsort(dst, stable=True)
        src = src[_o]
        dst = dst[_o]
        return (x, src, dst)
    x, src, dst = _rec_inputs()

    def _L0_gnn_setup():
        import jax, jax.numpy as jnp
        import numpy as np
        N, E, C = (50000, 9375, 128)
        BN_EPS = 1e-05
        NORM_EPS = 1e-12

        def _edgeconv(x, src, dst, wa, ba, g, be, rm, rv, wb, bb):
            x_i = x[dst]
            x_j = x[src]
            m = jnp.concatenate([x_i, x_j - x_i], axis=-1)
            m = jax.nn.relu(m @ wa.T + ba)
            m = (m - rm) * (g * jax.lax.rsqrt(rv + BN_EPS)) + be
            m = m @ wb.T + bb
            return jax.ops.segment_sum(m, dst, num_segments=x.shape[0])

        def _lin(k, fan_in, shape):
            bound = 1.0 / np.sqrt(fan_in)
            return jax.random.uniform(k, shape, jnp.float32, -bound, bound)
        key = jax.random.key(seed)
        ks = jax.random.split(key, 16)
        inp = {'x': jax.random.normal(ks[0], (N, C), jnp.float32), 'edge_index': jax.random.randint(ks[1], (2, E), 0, N, jnp.int64)}
        inp['w1a'] = _lin(ks[2], 2 * C, (C, 2 * C))
        inp['b1a'] = _lin(ks[3], 2 * C, (C,))
        inp['g1'] = jnp.ones((C,), jnp.float32) + 0.1 * jax.random.normal(ks[4], (C,))
        inp['be1'] = 0.1 * jax.random.normal(ks[5], (C,))
        inp['rm1'] = 0.1 * jax.random.normal(ks[6], (C,))
        inp['rv1'] = 0.5 + jax.random.uniform(ks[7], (C,))
        inp['w1b'] = _lin(ks[8], C, (C, C))
        inp['b1b'] = _lin(ks[9], C, (C,))
        inp['w2a'] = _lin(ks[10], 2 * C, (C, 2 * C))
        inp['b2a'] = _lin(ks[11], 2 * C, (C,))
        inp['g2'] = jnp.ones((C,), jnp.float32) + 0.1 * jax.random.normal(ks[12], (C,))
        inp['be2'] = 0.1 * jax.random.normal(ks[13], (C,))
        inp['rm2'] = 0.1 * jax.random.normal(ks[14], (C,))
        inp['rv2'] = 0.5 + jax.random.uniform(ks[15], (C,))
        k2 = jax.random.split(ks[15], 2)
        inp['w2b'] = _lin(k2[0], C, (C, C))
        inp['b2b'] = _lin(k2[1], C, (C,))
        return inp
    _L0_gnn_all = _L0_gnn_setup()
    _L0_gnn_in = {k: v for k, v in _L0_gnn_all.items() if k in ('w1a', 'b1a', 'g1', 'be1', 'rm1', 'rv1', 'w1b', 'b1b', 'w2a', 'b2a', 'g2', 'be2', 'rm2', 'rv2', 'w2b', 'b2b')}
    del _L0_gnn_all
    return {'x': x, 'src': src, 'dst': dst, 'L0_gnn_w1a': _L0_gnn_in['w1a'], 'L0_gnn_b1a': _L0_gnn_in['b1a'], 'L0_gnn_g1': _L0_gnn_in['g1'], 'L0_gnn_be1': _L0_gnn_in['be1'], 'L0_gnn_rm1': _L0_gnn_in['rm1'], 'L0_gnn_rv1': _L0_gnn_in['rv1'], 'L0_gnn_w1b': _L0_gnn_in['w1b'], 'L0_gnn_b1b': _L0_gnn_in['b1b'], 'L0_gnn_w2a': _L0_gnn_in['w2a'], 'L0_gnn_b2a': _L0_gnn_in['b2a'], 'L0_gnn_g2': _L0_gnn_in['g2'], 'L0_gnn_be2': _L0_gnn_in['be2'], 'L0_gnn_rm2': _L0_gnn_in['rm2'], 'L0_gnn_rv2': _L0_gnn_in['rv2'], 'L0_gnn_w2b': _L0_gnn_in['w2b'], 'L0_gnn_b2b': _L0_gnn_in['b2b']}

def reference(x, src, dst, L0_gnn_w1a, L0_gnn_b1a, L0_gnn_g1, L0_gnn_be1, L0_gnn_rm1, L0_gnn_rv1, L0_gnn_w1b, L0_gnn_b1b, L0_gnn_w2a, L0_gnn_b2a, L0_gnn_g2, L0_gnn_be2, L0_gnn_rm2, L0_gnn_rv2, L0_gnn_w2b, L0_gnn_b2b):
    import jax
    import jax.numpy as jnp

    def _L0_gnn_ref(x, edge_index, w1a, b1a, g1, be1, rm1, rv1, w1b, b1b, w2a, b2a, g2, be2, rm2, rv2, w2b, b2b):
        import jax, jax.numpy as jnp
        import numpy as np
        N, E, C = (50000, 9375, 128)
        BN_EPS = 1e-05
        NORM_EPS = 1e-12

        def _edgeconv(x, src, dst, wa, ba, g, be, rm, rv, wb, bb):
            x_i = x[dst]
            x_j = x[src]
            m = jnp.concatenate([x_i, x_j - x_i], axis=-1)
            m = jax.nn.relu(m @ wa.T + ba)
            m = (m - rm) * (g * jax.lax.rsqrt(rv + BN_EPS)) + be
            m = m @ wb.T + bb
            return jax.ops.segment_sum(m, dst, num_segments=x.shape[0])

        def _lin(k, fan_in, shape):
            bound = 1.0 / np.sqrt(fan_in)
            return jax.random.uniform(k, shape, jnp.float32, -bound, bound)
        src, dst = (edge_index[0], edge_index[1])
        h = _edgeconv(x, src, dst, w1a, b1a, g1, be1, rm1, rv1, w1b, b1b)
        h = jax.nn.relu(h)
        h = h / jnp.maximum(jnp.linalg.norm(h, axis=-1, keepdims=True), NORM_EPS)
        return _edgeconv(h, src, dst, w2a, b2a, g2, be2, rm2, rv2, w2b, b2b)
    edge_index = jnp.stack([src, dst])
    x = _layernorm(x + _L0_gnn_ref(x, edge_index, L0_gnn_w1a, L0_gnn_b1a, L0_gnn_g1, L0_gnn_be1, L0_gnn_rm1, L0_gnn_rv1, L0_gnn_w1b, L0_gnn_b1b, L0_gnn_w2a, L0_gnn_b2a, L0_gnn_g2, L0_gnn_be2, L0_gnn_rm2, L0_gnn_rv2, L0_gnn_w2b, L0_gnn_b2b), axis=-1)
    return x

_drawn_inputs = setup_inputs


def setup_inputs(seed=0):
    import zlib

    import numpy as np

    out = dict(_drawn_inputs(seed))
    spreads = {}
    factors = {'L0_gnn_w1a': 3.807,
     'L0_gnn_b1a': 8.0,
     'L0_gnn_g1': 8.0,
     'L0_gnn_be1': 8.0,
     'L0_gnn_rm1': 8.0,
     'L0_gnn_rv1': 8.0,
     'L0_gnn_w1b': 3.382,
     'L0_gnn_b1b': 8.0,
     'L0_gnn_w2a': 2.746,
     'L0_gnn_b2a': 3.126,
     'L0_gnn_g2': 7.302,
     'L0_gnn_rv2': 4.043}
    for name, (base, spread) in spreads.items():
        noise = np.random.default_rng([zlib.crc32(name.encode()), seed]).standard_normal(out[name].shape)
        drawn = base * np.exp(spread * noise) if base else spread * noise
        out[name] = jnp.asarray(drawn.astype(out[name].dtype))
    for name, factor in factors.items():
        out[name] = (out[name] * factor).astype(out[name].dtype)
    return out
```

```python
from contextlib import ExitStack

import concourse.bass as bass
from concourse import mybir

ALU = mybir.AluOpType
ACT = mybir.ActivationFunctionType
F32 = mybir.dt.float32
BF16 = mybir.dt.bfloat16
I32 = mybir.dt.int32

BN_EPS = 1e-5
LN_EPS = 1e-5
NORM_EPS = 1e-12

PN = 112
TILES = 3
SUB = PN * TILES
HALVES = 2
STEP = SUB * HALVES
SLOTS = 128
ROW = 125
WROWS = 5
WIN = ROW * WROWS


class Layer:

    def __init__(self, n, sems):
        self.n = n
        self.sems = sems

    def __getitem__(self, name):
        return self.sems[name]


def exists(i, back):
    return not isinstance(i, int) or i >= back


def gnn_kernel(nc, x, src, dst, weights, out):
    N, C = x.shape
    E = src.shape[0]
    ERWS = E // ROW
    STEPS = -(-N // STEP)
    NSUB = STEPS * HALVES
    SETS = -(-NSUB // 128)
    LAST = STEPS - 1
    assert E % ROW == 0 and C == 128 and STEPS % 2 == 1 and SUB + SLOTS + 1 <= WIN - ROW
    OVERLAP = STEPS * STEP - N
    assert OVERLAP % 2 == 0

    def node0(i):
        return N - STEP if isinstance(i, int) and i == LAST else i * STEP

    def rows_of(t, i):
        return t[bass.ds(node0(i), STEP), :].rearrange("(s p t) c -> p s (t c)", s=HALVES, t=TILES)

    acc_dram = nc.dram_tensor("acc_dram", (N, C), F32, kind="Internal").ap()
    P8, W8 = ERWS // 8, 8 * ROW
    assert N % P8 == 0
    h_dram = nc.dram_tensor("h_dram", (N, C), F32, kind="Internal").ap()
    src_rows = src.rearrange("(r e) -> r e", e=ROW)
    dst_rows = dst.rearrange("(r e) -> r e", e=ROW)

    with ExitStack() as ctx:
        def sb(name, shape, dt=F32):
            return ctx.enter_context(nc.sbuf_tensor(name, shape, dt))

        def sem(name):
            return ctx.enter_context(nc.semaphore(name))

        ident = sb("ident", [128, 128])
        ones_bf = sb("ones_bf", [128, 128], BF16)
        diff_iota = sb("diff_iota", [128, 128])
        node_iota = sb("node_iota", [128, TILES, PN])
        wa_raw = sb("wa_raw", [128, 2, 2 * C])
        wb_raw = sb("wb_raw", [128, 2, C])
        wl_t = sb("wl_t", [128, 2, C])
        wr_t = sb("wr_t", [128, 2, C])
        wd_t = sb("wd_t", [128, 2, C])
        wb_t = sb("wb_t", [128, 2, C])
        wp = sb("wp", [128, 2, C])
        cols = sb("cols", [128, 2, 5])
        bn_s = sb("bn_s", [128, 2])
        bn_t = sb("bn_t", [128, 2])
        bn_u = sb("bn_u", [128, 2])
        bb_row = sb("bb_row", [1, 2, C])
        v_row = sb("v_row", [1, 2, C])
        v_part = sb("v_part", [1, 3, 2, C], BF16)
        v_rest = sb("v_rest", [1, 2, 2, C])
        v_rows = sb("v_rows", [128, 2, C], BF16)
        row_first_i = sb("row_first_i", [128, 8], I32)
        row_first = sb("row_first", [128, 8])
        base_row = sb("base_row", [128, 128 * SETS])
        base_gap = sb("base_gap", [128, 128 * SETS])
        base_col = sb("base_col", [128, SETS])
        base_cgap = sb("base_cgap", [128, SETS])
        below = sb("below", [128, 8, 128 * SETS], BF16)
        win_row = sb("win_row", [128, SETS])
        win_idx = sb("win_idx", [128, SETS, WROWS], I32)
        win_src_i = sb("win_src_i", [128, SETS, WIN], I32)
        win_dst_i = sb("win_dst_i", [128, SETS, WIN], I32)
        win_src = sb("win_src", [128, SETS, WIN])
        win_dst = sb("win_dst", [128, SETS, WIN])
        win_a = sb("win_a", [128, SETS, WIN])
        win_b = sb("win_b", [128, SETS, WIN])
        packed = sb("packed", [128, SETS, WIN - 1], I32)
        found = sb("found", [128, SETS, 1 + SLOTS])
        found_i = sb("found_i", [128, 2, SETS, SLOTS], I32)
        found_f = sb("found_f", [128, 3, SETS, SLOTS])
        edge_idx = sb("edge_idx", [128, NSUB // 2, 4], I32)
        first_slot = sb("first_slot", [128, 1])
        edge_loc = sb("edge_loc", [128, 128 * SETS])
        x_in = sb("x_in", [PN, 2, HALVES, TILES * C])
        res_in = sb("res_in", [PN, 2, HALVES, TILES * C])
        idx_now = sb("idx_now", [128, 2, 4], I32)
        loc_now = sb("loc_now", [128, 2, HALVES])
        gathered = sb("gathered", [128, 2, 4, C])
        x_t = sb("x_t", [128, 2, STEP])
        g_t = sb("g_t", [128, 2, 4 * SLOTS])
        act_t = sb("act_t", [128, 2, STEP])
        msg_t = sb("msg_t", [128, 2, HALVES * SLOTS])
        msg_out = sb("msg_out", [128, 2, HALVES, C])
        onehot = sb("onehot", [128, 2, HALVES, SUB])
        z_relu = sb("z_relu", [PN, 2, HALVES * TILES, C])
        squares = sb("squares", [PN, 2, HALVES * TILES, C])
        sumsq = sb("sumsq", [PN, 2, HALVES * TILES])
        sumsq_min = sb("sumsq_min", [PN, 2, HALVES * TILES])
        root = sb("root", [PN, 2, HALVES * TILES])
        rinv = sb("rinv", [PN, 2, HALVES * TILES])
        y_out = sb("y_out", [PN, 2, HALVES * TILES, C])
        stats = sb("stats", [PN, 2, HALVES * TILES, 6])
        meanvar = sb("meanvar", [PN, 2, HALVES * TILES, 2])
        all_src_i = sb("all_src_i", [P8, W8], I32)
        all_dst_i = sb("all_dst_i", [P8, W8], I32)
        all_next_i = sb("all_next_i", [P8, W8], I32)
        all_src = sb("all_src", [P8, W8])
        all_dst = sb("all_dst", [P8, W8])
        all_next = sb("all_next", [P8, W8])
        all_flag = sb("all_flag", [P8, W8])
        faults = sb("faults", [128, 2 + SETS])
        faults_sum = sb("faults_sum", [1, 2 + SETS])
        faults_all = sb("faults_all", [1, 1])
        general_i = sb("general_i", [1, 1], I32)
        ones_f = sb("ones_f", [128, 1])
        zeros = sb("zeros", [PN, HALVES, TILES * C])
        before = sb("before", [128, 128])
        e_src_i = sb("e_src_i", [ROW, 1], I32)
        e_dst_i = sb("e_dst_i", [ROW, 1], I32)
        e_row_i = sb("e_row_i", [ROW, ROW], I32)
        e_dst = sb("e_dst", [ROW, 1])
        e_row = sb("e_row", [ROW, ROW])
        e_same = sb("e_same", [ROW, ROW])
        e_earlier = sb("e_earlier", [ROW, ROW])
        e_count = sb("e_count", [ROW, 1])
        e_skip = sb("e_skip", [ROW, 1])
        e_put = sb("e_put", [ROW, 1])
        e_put_i = sb("e_put_i", [ROW, 1], I32)
        e_rows = sb("e_rows", [ROW, 2, C])
        e_rows_t = sb("e_rows_t", [128, 2, 128])
        e_msg_t = sb("e_msg_t", [128, 128])
        e_out = sb("e_out", [ROW, C])
        e_acc = sb("e_acc", [ROW, C])
        e_new = sb("e_new", [ROW, C])
        ps_x = ctx.enter_context(nc.psum_tensor("ps_x", [128, HALVES, 512], F32))
        ps_u = ctx.enter_context(nc.psum_tensor("ps_u", [128, HALVES, 512], F32))
        ps_z = ctx.enter_context(nc.psum_tensor("ps_z", [128, HALVES, 512], F32))
        ps_g = ctx.enter_context(nc.psum_tensor("ps_g", [128, 512], F32))
        ps_e = ctx.enter_context(nc.psum_tensor("ps_e", [128, 512], F32))

        weights_loaded = sem("weights_loaded")
        first_loaded = sem("first_loaded")
        consts_made = sem("consts_made")
        dve_setup = sem("dve_setup")
        act_setup = sem("act_setup")
        w_turned = sem("w_turned")
        v_made = sem("v_made")
        v_split = sem("v_split")
        v_moved = sem("v_moved")
        rows_below = sem("rows_below")
        rows_counted = sem("rows_counted")
        win_idx_made = sem("win_idx_made")
        win_loaded = [sem(f"win_loaded{s}") for s in range(SETS)]
        found_made = sem("found_made")
        found_turned = sem("found_turned")
        index_made = sem("index_made")
        next_cleared = sem("next_cleared")
        all_loaded = sem("all_loaded")
        faults_counted = sem("faults_counted")
        faults_summed = sem("faults_summed")
        path_chosen = sem("path_chosen")

        def layer(n):
            L = Layer(n, {what: sem(f"{what}_{n}") for what in (
                    "idx_staged", "gathers_begun",
                    "xt_ps", "gt_ps", "u_ps", "pre_ps", "mout_ps", "z0_ps", "z1_ps",
                    "xt_made", "loc_made", "onehot_made", "mout_made",
                    "sums_made", "sums_begun", "sums_min", "rinv_made", "out_made", "z0_added", "z1_added",
                    "gt_made", "act_made", "msg_made", "z0_relued", "z1_relued", "root_made")})
            L.sems["x_loaded"] = [sem(f"x_loaded_{n}_{s}") for s in range(2)]
            L.sems["res_loaded"] = [sem(f"res_loaded_{n}_{s}") for s in range(2)]
            L.sems["rows_gathered"] = [sem(f"rows_gathered_{n}_{s}") for s in range(2)]
            L.sems["stored"] = [sem(f"stored_{n}_{s}") for s in range(2)]
            L.sems["z_read"] = (L["z0_relued"], L["z1_relued"]) if n == 0 else (L["z0_added"], L["z1_added"])
            L.sems["z_ps"] = (L["z0_ps"], L["z1_ps"])
            return L

        layers = [layer(0), layer(1)]
        IN = (x, h_dram)
        OUT = (h_dram, out)

        def general_layer(n):
            return Layer(n, {what: sem(f"{what}_{n}") for what in (
                "g_cleared", "g_begun", "g_ended", "g_edges_loaded", "g_rows_gathered", "g_acc_gathered", "g_scattered",
                "g_turned", "g_turned_made", "g_pre", "g_msg_made", "g_mout", "g_mout_made", "g_sum",
                "g_sum_made", "g_dve", "g_acc_loaded", "g_node_dve", "g_sums_made", "g_root_made",
                "g_out_made", "g_stored")})

        general = [general_layer(0), general_layer(1)]

        def takes_general_path(eng):
            eng.wait_ge(layers[1]["stored"][0], loads(LAST))
            eng.wait_ge(layers[1]["stored"][1], loads(LAST - 1))
            eng.wait_ge(path_chosen, 1)
            return eng.value_load(general_i[0:1, 0:1], min_val=0, max_val=1)

        def loads(i):
            return (i // 2 + 1) * 16

        def slot_loads(i, slot):
            return loads(i) if isinstance(i, int) else (i - slot) * 8 + 16

        def over_steps(eng, step):
            step(0, 0)
            step(1, 1)
            with eng.Fori(2, LAST - 1, 2) as i:
                step(i, 0)
                step(i + 1, 1)

        def over_nodes(eng):
            with eng.Fori(0, LAST) as i:
                yield i
            yield LAST

        block = ctx.enter_context(nc.Block())

        @block.sync
        def _(sp):
            sp.dma_start(row_first_i[0:ERWS // 8, :],
                         dst.rearrange("(p c e) -> p c e", c=8, e=ROW)[:, :, 0],
                         allow_slow_non_contiguous=True).then_inc(first_loaded, 16)
            sp.wait_ge(next_cleared, 1)
            sp.dma_start(all_src_i[:], src.rearrange("(p w) -> p w", w=W8)).then_inc(all_loaded, 16)
            sp.dma_start(all_dst_i[:], dst.rearrange("(p w) -> p w", w=W8)).then_inc(all_loaded, 16)
            sp.dma_start(all_next_i[0:P8 - 1, :], dst[1:E - W8 + 1].rearrange("(p w) -> p w", w=W8)).then_inc(all_loaded, 16)
            sp.dma_start(all_next_i[P8 - 1:P8, 0:W8 - 1],
                         dst[E - W8 + 1:E].rearrange("(p w) -> p w", p=1)).then_inc(all_loaded, 16)
            for n, w in enumerate(weights):
                sp.dma_start(wa_raw[:, n, :], w["wa"]).then_inc(weights_loaded, 16)
                sp.dma_start(wb_raw[:, n, :], w["wb"]).then_inc(weights_loaded, 16)
                sp.dma_start(bb_row[0:1, n, :], w["bb"].rearrange("(a c) -> a c", a=1)).then_inc(weights_loaded, 16)
                for k, name in enumerate(("ba", "g", "be", "rm", "rv")):
                    sp.dma_start(cols[:, n, k:k + 1], w[name].rearrange("(c a) -> c a", a=1),
                                 allow_slow_non_contiguous=True).then_inc(weights_loaded, 16)
            sp.wait_ge(v_split, 1)
            for k in range(3):
                sp.dma_start(v_rows[k:k + 1, :, :], v_part[0:1, k, :, :]).then_inc(v_moved, 16)

            for L in layers:
                if L.n == 1:
                    sp.wait_ge(layers[0]["stored"][0], loads(LAST))
                    sp.wait_ge(layers[0]["stored"][1], loads(LAST - 1))

                def load(i, slot):
                    if exists(i, 2):
                        sp.wait_ge(L["xt_ps"], i - 1)
                    sp.dma_start(x_in[:, slot, :, :], rows_of(IN[L.n], i)).then_inc(L["x_loaded"][slot], 16)
                    if L.n == 1:
                        if exists(i, 2):
                            sp.wait_ge(L["z1_added"], i - 1)
                        sp.dma_start(res_in[:, slot, :, :], rows_of(x, i)).then_inc(L["res_loaded"][slot], 16)

                def store(i, slot):
                    sp.wait_ge(L["out_made"], i + 1)
                    if isinstance(i, int) and i == LAST:
                        sp.wait_ge(L["stored"][1], loads(LAST - 1))
                    sp.dma_start(rows_of(OUT[L.n], i),
                                 y_out[:, slot, :, :].rearrange("p (s t) c -> p s (t c)", s=HALVES)
                                 ).then_inc(L["stored"][slot], 16)

                def step(i, slot):
                    load(i, slot)
                    if exists(i, 3):
                        store(i - 3, 1 - slot)

                step(0, 0)
                step(1, 1)
                step(2, 0)
                step(3, 1)
                with sp.Fori(4, LAST - 1, 2) as i:
                    step(i, 0)
                    step(i + 1, 1)
                step(LAST, 0)
                for i in (LAST - 2, LAST - 1, LAST):
                    store(i, i % 2)

            with sp.If(takes_general_path(sp)):
                for G in general:
                    if G.n == 1:
                        sp.wait_ge(general[0]["g_stored"], 16 * STEPS)
                    for i in over_nodes(sp):
                        sp.dma_start(rows_of(acc_dram, i), zeros[:]).then_inc(G["g_cleared"], 16)
                        sp.wait_ge(G["g_cleared"], i * 16 + 16)
                        sp.sem_inc(G["g_ended"], 1)
                    with sp.Fori(0, ERWS) as r:
                        def edges(t, p):
                            return t[bass.ds(r, 1), :].rearrange("r e -> e r" if p == 1 else "r e -> r e")
                        sp.dma_start(e_src_i[:], edges(src_rows, 1), allow_slow_non_contiguous=True
                                     ).then_inc(G["g_edges_loaded"], 16)
                        sp.dma_start(e_dst_i[:], edges(dst_rows, 1), allow_slow_non_contiguous=True
                                     ).then_inc(G["g_edges_loaded"], 16)
                        sp.dma_start(e_row_i[:], edges(dst_rows, 0).to_broadcast([ROW, ROW])
                                     ).then_inc(G["g_edges_loaded"], 16)
                        sp.wait_ge(G["g_scattered"], r * 16 + 16)
                        sp.sem_inc(G["g_ended"], 1)
                    for i in over_nodes(sp):
                        sp.dma_start(x_in[:, 0, :, :], rows_of(acc_dram, i)).then_inc(G["g_acc_loaded"], 16)
                        sp.dma_start(res_in[:, 0, :, :], rows_of(x, i)).then_inc(G["g_acc_loaded"], 16)
                        sp.wait_ge(G["g_out_made"], i + 1)
                        sp.dma_start(rows_of(OUT[G.n], i),
                                     y_out[:, 0, :, :].rearrange("p (s t) c -> p s (t c)", s=HALVES)
                                     ).then_inc(G["g_stored"], 16)
                        sp.wait_ge(G["g_stored"], i * 16 + 16)
                        sp.sem_inc(G["g_ended"], 1)

        @block.gpsimd
        def _(pool):
            nc.gpsimd.iota(diff_iota[:], [[1, 128]], base=0, channel_multiplier=-1,
                           allow_small_or_imprecise_dtypes=True)
            nc.gpsimd.iota(base_row[:], [[SUB, 128 * SETS]], base=0, channel_multiplier=0,
                           allow_small_or_imprecise_dtypes=True)
            for s in range(SETS):
                nc.gpsimd.iota(base_col[:, s:s + 1], [[0, 1]], base=SUB * 128 * s, channel_multiplier=SUB,
                               allow_small_or_imprecise_dtypes=True)
            nc.gpsimd.iota(node_iota[:], [[1, TILES], [TILES, PN]], base=0, channel_multiplier=0,
                           allow_small_or_imprecise_dtypes=True).then_inc(consts_made, 1)

            pool.wait_ge(win_idx_made, 1)
            for s in range(SETS):
                for r in range(WROWS):
                    for rows, win in ((src_rows, win_src_i), (dst_rows, win_dst_i)):
                        nc.gpsimd.indirect_dma_start(
                            out=win[:, s, r * ROW:(r + 1) * ROW], out_offset=None, in_=rows,
                            in_offset=bass.IndirectOffsetOnAxis(ap=win_idx[:, s, r:r + 1], axis=0),
                        ).then_inc(win_loaded[s], 16)

            pool.wait_ge(index_made, 3)
            for L in layers:
                if L.n == 1:
                    pool.wait_ge(layers[0]["stored"][0], loads(LAST))
                    pool.wait_ge(layers[0]["stored"][1], loads(LAST - 1))

                def gather(i, slot):
                    if exists(i, 2):
                        pool.wait_ge(L["rows_gathered"][slot], slot_loads(i, slot) * 4 - 64)
                    nc.gpsimd.tensor_copy(idx_now[:, slot, :], edge_idx[:, bass.ds(i, 1), :].rearrange(
                        "p i k -> p (i k)")).then_inc(L["idx_staged"], 1)
                    if exists(i, 2):
                        pool.wait_ge(L["gt_ps"], i - 1)
                    pool.wait_ge(L["idx_staged"], i + 1)
                    pool.sem_inc(L["gathers_begun"], 1)
                    for k in range(4):
                        nc.gpsimd.indirect_dma_start(
                            out=gathered[:, slot, k, :], out_offset=None, in_=IN[L.n],
                            in_offset=bass.IndirectOffsetOnAxis(ap=idx_now[:, slot, k:k + 1], axis=0),
                        ).then_inc(L["rows_gathered"][slot], 16)

                over_steps(pool, gather)
                gather(LAST, 0)

            with pool.If(takes_general_path(pool)):
                for G in general:
                    pool.wait_ge(G["g_cleared"], 16 * STEPS)
                    with pool.Fori(0, ERWS) as r:
                        pool.wait_ge(G["g_edges_loaded"], r * 48 + 48)
                        pool.sem_inc(G["g_begun"], 1)
                        for k, idx in enumerate((e_src_i, e_dst_i)):
                            nc.gpsimd.indirect_dma_start(
                                out=e_rows[:, k, :], out_offset=None, in_=IN[G.n],
                                in_offset=bass.IndirectOffsetOnAxis(ap=idx[:, 0:1], axis=0),
                            ).then_inc(G["g_rows_gathered"], 16)
                        nc.gpsimd.indirect_dma_start(
                            out=e_acc[:], out_offset=None, in_=acc_dram,
                            in_offset=bass.IndirectOffsetOnAxis(ap=e_dst_i[:, 0:1], axis=0),
                        ).then_inc(G["g_acc_gathered"], 16)
                        pool.wait_ge(G["g_sum_made"], r + 1)
                        pool.sem_inc(G["g_begun"], 1)
                        nc.gpsimd.indirect_dma_start(
                            out=acc_dram, out_offset=bass.IndirectOffsetOnAxis(ap=e_put_i[:, 0:1], axis=0),
                            in_=e_new[:], in_offset=None, bounds_check=N - 1, oob_is_err=False,
                        ).then_inc(G["g_scattered"], 16)
                        pool.wait_ge(G["g_scattered"], r * 16 + 16)

        @block.tensor
        def _(pe):
            pe.wait_ge(weights_loaded, 16 * 16)
            pe.wait_ge(dve_setup, 1)
            for n in range(2):
                for k, w in enumerate((wa_raw[:, n, 0:C], wa_raw[:, n, C:2 * C], wb_raw[:, n, :])):
                    last = nc.tensor.transpose(ps_x[:, n, k * C:(k + 1) * C], w, ident[:])
            last.then_inc(w_turned, 1)
            pe.wait_ge(rows_below, 1)
            for s in range(SETS):
                for c in range(8):
                    last = nc.tensor.matmul(ps_g[:, s:s + 1], below[0:ERWS // 8, c, s * 128:(s + 1) * 128],
                                            ones_bf[0:ERWS // 8, 0:1], start=(c == 0), stop=(c == 7))
            last.then_inc(rows_counted, 1)
            pe.wait_ge(v_made, 1)
            for n in range(2):
                last = nc.tensor.matmul(ps_u[0:1, n, 0:C], bn_t[:, n:n + 1], wb_t[:, n, :], start=True, stop=True)
            last.then_inc(v_made, 1)
            pe.wait_ge(found_made, 1)
            for k, ps in enumerate((ps_x[:, 0, :], ps_x[:, 1, :], ps_g)):
                for s in range(SETS):
                    last = nc.tensor.transpose(ps[:, s * 128:(s + 1) * 128], found_f[:, k, s, :], ident[:])
            last.then_inc(found_turned, 1)
            pe.wait_ge(faults_counted, 1)
            nc.tensor.matmul(ps_e[0:1, 0:2 + SETS], ones_f[:], faults[:], start=True, stop=True).then_inc(faults_summed, 1)
            pe.wait_ge(path_chosen, 1)
            pe.wait_ge(v_moved, 48)
            pe.wait_ge(index_made, 3)

            for L in layers:
                n = L.n

                def turn(i, slot):
                    pe.wait_ge(L["x_loaded"][slot], slot_loads(i, slot))
                    if n == 1 and isinstance(i, int) and i == 0:
                        pe.wait_ge(layers[0]["xt_made"], STEPS)
                    for s in range(HALVES):
                        for t in range(TILES):
                            last = nc.tensor.transpose(ps_x[:, s, t * PN:(t + 1) * PN],
                                                       x_in[:, slot, s, t * C:(t + 1) * C], ident[0:PN, 0:PN])
                    last.then_inc(L["xt_ps"], 1)
                    pe.wait_ge(L["rows_gathered"][slot], slot_loads(i, slot) * 4)
                    for k in range(4):
                        last = nc.tensor.transpose(ps_g[:, k * SLOTS:(k + 1) * SLOTS], gathered[:, slot, k, :], ident[:])
                    last.then_inc(L["gt_ps"], 1)

                def first_products(i, slot):
                    pe.wait_ge(L["xt_made"], i + 1)
                    for s in range(HALVES):
                        last = nc.tensor.matmul(ps_u[:, s, 0:SUB], wl_t[:, n, :], x_t[:, slot, s * SUB:(s + 1) * SUB],
                                                start=True, stop=True)
                    last.then_inc(L["u_ps"], 1)
                    pe.wait_ge(L["gt_made"], i + 1)
                    pre = ps_e[:, 0:HALVES * SLOTS]
                    nc.tensor.matmul(pre, wr_t[:, n, :], g_t[:, slot, 0:2 * SLOTS], start=True, stop=False)
                    nc.tensor.matmul(pre, wd_t[:, n, :], g_t[:, slot, 2 * SLOTS:], start=False,
                                     stop=True).then_inc(L["pre_ps"], 1)

                def message_products(i, slot):
                    pe.wait_ge(L["msg_made"], i + 1)
                    for s in range(HALVES):
                        o = ps_e[:, (2 + s) * C:(3 + s) * C]
                        nc.tensor.matmul(o, msg_t[:, slot, s * SLOTS:(s + 1) * SLOTS], wp[:, n, :], start=True, stop=False)
                        last = nc.tensor.matmul(o, ones_bf[:], v_rows[:, n, :], start=False, stop=True)
                    last.then_inc(L["mout_ps"], 1)

                def node_products(i, slot, s):
                    if s == 0:
                        pe.wait_ge(L["act_made"], i + 1)
                        pe.wait_ge(L["onehot_made"], i + 1)
                        pe.wait_ge(L["mout_made"], i + 1)
                    if exists(i, 1):
                        pe.wait_ge(L["z_read"][s], i)
                    for t in range(TILES):
                        o = ps_z[0:PN, s, t * C:(t + 1) * C]
                        at = s * SUB + t * PN
                        nc.tensor.matmul(o, act_t[:, slot, at:at + PN], wp[:, n, :], start=True, stop=False)
                        last = nc.tensor.matmul(o, onehot[:, slot, s, t * PN:(t + 1) * PN], msg_out[:, slot, s, :],
                                                start=False, stop=True)
                    last.then_inc(L["z_ps"][s], 1)

                def step(i, slot):
                    turn(i + 1, 1 - slot)
                    node_products(i, slot, 0)
                    first_products(i + 1, 1 - slot)
                    node_products(i, slot, 1)
                    message_products(i + 1, 1 - slot)

                turn(0, 0)
                first_products(0, 0)
                message_products(0, 0)
                over_steps(pe, step)
                node_products(LAST, 0, 0)
                node_products(LAST, 0, 1)

            with pe.If(takes_general_path(pe)):
                for G in general:
                    n = G.n
                    with pe.Fori(0, ERWS) as r:
                        pe.wait_ge(G["g_rows_gathered"], r * 32 + 32)
                        for k in range(2):
                            last = nc.tensor.transpose(ps_g[:, k * 128:k * 128 + ROW], e_rows[:, k, :], ident[0:ROW, 0:ROW])
                        last.then_inc(G["g_turned"], 1)
                        pe.wait_ge(G["g_turned_made"], r + 1)
                        nc.tensor.matmul(ps_e[:, 0:ROW], wr_t[:, n, :], e_rows_t[:, 0, 0:ROW], start=True, stop=False)
                        nc.tensor.matmul(ps_e[:, 0:ROW], wd_t[:, n, :], e_rows_t[:, 1, 0:ROW], start=False,
                                         stop=True).then_inc(G["g_pre"], 1)
                        pe.wait_ge(G["g_msg_made"], r + 1)
                        nc.tensor.matmul(ps_u[0:ROW, 0, 0:C], e_msg_t[:, 0:ROW], wp[:, n, :], start=True, stop=False)
                        nc.tensor.matmul(ps_u[0:ROW, 0, 0:C], ones_bf[:, 0:ROW], v_rows[:, n, :], start=False,
                                         stop=True).then_inc(G["g_mout"], 1)
                        pe.wait_ge(G["g_mout_made"], r + 1)
                        nc.tensor.matmul(ps_z[0:ROW, 0, 0:C], e_same[:], e_out[:], start=True,
                                         stop=True).then_inc(G["g_sum"], 1)

        @block.scalar
        def _(act):
            act.wait_ge(act_setup, 1)
            nc.scalar.activation(bn_t[:], bn_u[:], ACT.Sqrt).then_inc(act_setup, 1)

            for L in layers:
                n = L.n
                bias = cols[:, n, 0:1]

                def turn(i, slot):
                    act.wait_ge(L["xt_ps"], i + 1)
                    nc.scalar.activation(x_t[:, slot, :].rearrange("p (s c) -> p s c", s=HALVES),
                                         ps_x[:, :, 0:SUB], ACT.Copy).then_inc(L["xt_made"], 1)
                    act.wait_ge(L["gt_ps"], i + 1)
                    nc.scalar.activation(g_t[:, slot, :], ps_g[:], ACT.Copy).then_inc(L["gt_made"], 1)

                def relu_nodes(i, slot):
                    act.wait_ge(L["u_ps"], i + 1)
                    nc.scalar.activation(act_t[:, slot, :].rearrange("p (s c) -> p s c", s=HALVES), ps_u[:, :, 0:SUB],
                                         ACT.Relu, bias=bias).then_inc(L["act_made"], 1)
                    act.wait_ge(L["pre_ps"], i + 1)
                    nc.scalar.activation(msg_t[:, slot, :].rearrange("p (s e) -> p s e", s=HALVES)[:, :, 1:],
                                         ps_e[:, 0:HALVES * SLOTS].rearrange("p (s e) -> p s e", s=HALVES)[:, :, 1:],
                                         ACT.Relu, bias=bias).then_inc(L["msg_made"], 1)

                def relu_out(i, slot, s):
                    act.wait_ge(L["z_ps"][s], i + 1)
                    if exists(i, 2) and s == 0:
                        act.wait_ge(L["out_made"], i - 1)
                    nc.scalar.activation(z_relu[:, slot, s * TILES:(s + 1) * TILES, :].rearrange("p t c -> p (t c)"),
                                         ps_z[0:PN, s, 0:TILES * C], ACT.Relu).then_inc(L["z_read"][s], 1)

                def root_of(i, slot):
                    act.wait_ge(L["sums_min"], i + 1)
                    nc.scalar.activation(root[:, slot, :], sumsq_min[:, slot, :], ACT.Sqrt).then_inc(L["root_made"], 1)

                def step(i, slot):
                    turn(i + 1, 1 - slot)
                    if exists(i, 1):
                        root_of(i - 1, 1 - slot)
                    if n == 0:
                        relu_out(i, slot, 0)
                    relu_nodes(i + 1, 1 - slot)
                    if n == 0:
                        relu_out(i, slot, 1)

                turn(0, 0)
                relu_nodes(0, 0)
                over_steps(act, step)
                root_of(LAST - 1, 1)
                if n == 0:
                    relu_out(LAST, 0, 0)
                    relu_out(LAST, 0, 1)
                root_of(LAST, 0)

            with act.If(takes_general_path(act)):
                for G in general:
                    with act.Fori(0, ERWS) as r:
                        act.wait_ge(G["g_turned"], r + 1)
                        nc.scalar.activation(e_rows_t[:, :, 0:ROW], ps_g[:, 0:256].rearrange(
                            "p (k e) -> p k e", k=2)[:, :, 0:ROW], ACT.Copy).then_inc(G["g_turned_made"], 1)
                        act.wait_ge(G["g_pre"], r + 1)
                        nc.scalar.activation(e_msg_t[:, 0:ROW], ps_e[:, 0:ROW], ACT.Relu,
                                             bias=cols[:, G.n, 0:1]).then_inc(G["g_msg_made"], 1)
                    for i in over_nodes(act):
                        act.wait_ge(G["g_sums_made"], i + 1)
                        nc.scalar.activation(root[:, 0, :], sumsq_min[:, 0, :], ACT.Sqrt).then_inc(G["g_root_made"], 1)

        @block.vector
        def _(dve):
            done = [0]

            def link(ins):
                done[0] += 1
                ins.then_inc(dve_setup, 1)
                dve.wait_ge(dve_setup, done[0])

            V = nc.vector
            dve.wait_ge(consts_made, 1)
            V.memset(all_next_i[:], N).then_inc(next_cleared, 1)
            V.memset(ones_bf[:], 1.0)
            V.memset(ones_f[:], 1.0)
            V.memset(zeros[:], 0.0)
            V.memset(found[:, :, 0:1], 0.0)
            V.memset(msg_t[:], 0.0)
            V.tensor_scalar(first_slot[:], diff_iota[:, 0:1], 0.0, None, ALU.is_equal)
            V.memset(faults[:], 0.0)
            V.tensor_scalar(before[:], diff_iota[:], 0.0, None, ALU.is_lt)
            V.memset(v_rows[:], 0.0)
            link(V.tensor_scalar(ident[:], diff_iota[:], 0.0, None, ALU.is_equal))
            for v, gap in ((base_row, base_gap), (base_col, base_cgap)):
                link(V.tensor_scalar(gap[:], v[:], float(LAST * STEP), -float(OVERLAP), ALU.is_ge, ALU.mult))
                link(V.tensor_tensor(gap[:], gap[:], v[:], ALU.add))
                link(V.tensor_scalar(v[:], gap[:], float(N - SUB), None, ALU.min))
            dve.wait_ge(first_loaded, 16)
            q = ERWS // 8
            link(V.tensor_copy(row_first[0:q, :], row_first_i[0:q, :]))
            for c in range(8):
                last = V.tensor_scalar(below[0:q, c, :], base_row[0:q, :], row_first[0:q, c:c + 1], None, ALU.is_gt)
            last.then_inc(rows_below, 1)
            dve.wait_ge(rows_counted, 1)
            link(V.tensor_scalar(win_row[:], ps_g[:, 0:SETS], 1.0, 0.0, ALU.subtract, ALU.max))
            link(V.tensor_scalar(win_row[:], win_row[:], float(ERWS - WROWS), None, ALU.min))
            for r in range(WROWS):
                last = V.tensor_scalar(win_idx[:, :, r], win_row[:], float(r), None, ALU.add)
            last.then_inc(win_idx_made, 1)

            dve.wait_ge(all_loaded, 64)
            V.tensor_copy(all_src[:], all_src_i[:])
            V.tensor_copy(all_dst[:], all_dst_i[:])
            link(V.tensor_copy(all_next[:], all_next_i[:]))
            V.tensor_tensor(all_src[:], all_src[:], all_dst[:], ALU.is_equal)
            link(V.tensor_tensor(all_next[:], all_next[:], all_dst[:], ALU.subtract))
            link(V.tensor_scalar(all_dst[:], all_next[:], 0.0, None, ALU.is_gt))
            V.tensor_tensor_reduce(all_flag[:], all_src[:], all_dst[:], 1.0, 0.0, ALU.mult, ALU.add, faults[0:P8, 1:2])
            link(V.tensor_scalar(all_next[:], all_next[:], 0.0, None, ALU.is_lt))
            V.tensor_reduce(faults[0:P8, 0:1], all_next[:], mybir.AxisListType.X, ALU.add)
            link(V.tensor_scalar(faults[0:P8, 1:2], faults[0:P8, 1:2], float(N // P8), None, ALU.subtract))

            dve.wait_ge(weights_loaded, 16 * 16)
            V.tensor_scalar(bn_u[:], cols[:, :, 4], BN_EPS, None, ALU.add).then_inc(act_setup, 1)
            dve.wait_ge(w_turned, 1)
            for n in range(2):
                for k, w in enumerate((wl_t, wr_t, wb_t)):
                    last = V.tensor_copy(w[:, n, :], ps_x[:, n, k * C:(k + 1) * C])
            link(last)
            dve.wait_ge(act_setup, 2)
            link(V.reciprocal(bn_u[:], bn_t[:]))
            link(V.tensor_tensor(bn_s[:], bn_u[:], cols[:, :, 1], ALU.mult))
            link(V.tensor_tensor(bn_u[:], bn_s[:], cols[:, :, 3], ALU.mult))
            V.tensor_tensor(bn_t[:], cols[:, :, 2], bn_u[:], ALU.subtract).then_inc(v_made, 1)
            for n in range(2):
                V.tensor_tensor(wd_t[:, n, :], wl_t[:, n, :], wr_t[:, n, :], ALU.subtract)
                V.tensor_scalar(wp[:, n, :], wb_t[:, n, :], bn_s[:, n:n + 1], None, ALU.mult)
            dve.wait_ge(v_made, 2)
            link(V.tensor_tensor(v_row[:], ps_u[0:1, :, 0:C], bb_row[:], ALU.add))
            link(V.tensor_copy(v_part[0:1, 0], v_row[:]))
            link(V.tensor_tensor(v_rest[0:1, 0], v_row[:], v_part[0:1, 0], ALU.subtract))
            link(V.tensor_copy(v_part[0:1, 1], v_rest[0:1, 0]))
            link(V.tensor_tensor(v_rest[0:1, 1], v_rest[0:1, 0], v_part[0:1, 1], ALU.subtract))
            V.tensor_copy(v_part[0:1, 2], v_rest[0:1, 1]).then_inc(v_split, 1)

            M = WIN - 1
            for s in range(SETS):
                dve.wait_ge(win_loaded[s], 2 * WROWS * 16)
                V.tensor_copy(win_src[:, s, :], win_src_i[:, s, :])
                link(V.tensor_copy(win_dst[:, s, :], win_dst_i[:, s, :]))
                link(V.tensor_tensor(win_a[:, s, 0:M], win_dst[:, s, 0:M], win_dst[:, s, 1:], ALU.not_equal))
                link(V.tensor_tensor(win_b[:, s, 0:M], win_dst[:, s, 0:M], win_src[:, s, 0:M], ALU.is_equal))
                link(V.tensor_tensor(win_b[:, s, 0:M], win_a[:, s, 0:M], win_b[:, s, 0:M], ALU.mult))
                link(V.tensor_scalar(win_a[:, s, 0:M], win_b[:, s, 0:M], -1.0, 1.0, ALU.mult, ALU.add))
                link(V.tensor_scalar(win_dst[:, s, 0:M], win_dst[:, s, 0:M], base_col[:, s:s + 1], None, ALU.subtract))
                link(V.scalar_tensor_tensor(win_b[:, s, 0:M], win_dst[:, s, 0:M], 0.0, win_a[:, s, 0:M],
                                            ALU.is_ge, ALU.mult))
                link(V.scalar_tensor_tensor(win_a[:, s, 0:M], win_dst[:, s, 0:M], float(SUB), win_b[:, s, 0:M],
                                            ALU.is_lt, ALU.mult))
                V.scalar_tensor_tensor(win_dst_i[:, s, 0:M], win_dst[:, s, 0:M], 2049.0, win_a[:, s, 0:M],
                                       ALU.add, ALU.mult)
                link(V.tensor_tensor(win_src_i[:, s, 0:M], win_src[:, s, 0:M], win_a[:, s, 0:M], ALU.mult))
                link(V.scalar_tensor_tensor(packed[:, s, :], win_dst_i[:, s, 0:M], 17, win_src_i[:, s, 0:M],
                                            ALU.logical_shift_left, ALU.bitwise_or))
            start = done[0]
            for r in range(SLOTS // 8):
                for s in range(SETS):
                    if r:
                        dve.wait_ge(dve_setup, start + (2 * r - 1) * SETS + s + 1)
                    V.max(found[:, s, 8 * r + 1:8 * r + 9], packed[:, s, :].bitcast(F32)).then_inc(dve_setup, 1)
                for s in range(SETS):
                    dve.wait_ge(dve_setup, start + 2 * r * SETS + s + 1)
                    V.match_replace(packed[:, s, :].bitcast(F32), found[:, s, 8 * r + 1:8 * r + 9],
                                    packed[:, s, :].bitcast(F32), 0.0).then_inc(dve_setup, 1)
            done[0] = start + 2 * SETS * SLOTS // 8
            dve.wait_ge(dve_setup, done[0])
            for s in range(SETS):
                last = V.tensor_reduce(faults[:, 2 + s:3 + s], packed[:, s, :].bitcast(F32), mybir.AxisListType.X, ALU.max)
            link(last)
            V.tensor_tensor(faults[:, 2:], faults[:, 2:], found[:, :, SLOTS], ALU.max)
            bits = found[:, :, 0:SLOTS].bitcast(I32)
            V.tensor_scalar(found_i[:, 0], bits, (1 << 17) - 1, None, ALU.bitwise_and)
            link(V.tensor_scalar(found_i[:, 1], bits, 17, 2047, ALU.logical_shift_right, ALU.bitwise_and))
            V.tensor_copy(found_f[:, 0], found_i[:, 0])
            link(V.tensor_scalar(found_f[:, 1], found_i[:, 1], 1.0, None, ALU.subtract))
            for s in range(SETS):
                last = V.tensor_scalar(found_f[:, 2, s, :], found_f[:, 1, s, :], 0.0, base_col[:, s:s + 1],
                                       ALU.max, ALU.add)
            last.then_inc(found_made, 1)
            V.tensor_scalar(faults[:, 2:], faults[:, 2:], 0.0, None, ALU.is_gt).then_inc(faults_counted, 1)
            dve.wait_ge(found_turned, 1)
            V.tensor_copy(edge_idx[:, :, 0:2], ps_x[:, 0, 0:NSUB].rearrange("p (i h) -> p i h", h=2)).then_inc(index_made, 1)
            V.tensor_copy(edge_idx[:, :, 2:4], ps_g[:, 0:NSUB].rearrange("p (i h) -> p i h", h=2)).then_inc(index_made, 1)
            V.tensor_copy(edge_loc[:, 0:NSUB], ps_x[:, 1, 0:NSUB]).then_inc(index_made, 1)
            dve.wait_ge(index_made, 3)
            dve.wait_ge(faults_summed, 1)
            link(V.tensor_copy(faults_sum[:], ps_e[0:1, 0:2 + SETS]))
            link(V.tensor_tensor(faults_sum[:], faults_sum[:], faults_sum[:], ALU.mult))
            link(V.tensor_reduce(faults_all[:], faults_sum[:], mybir.AxisListType.X, ALU.max))
            V.tensor_scalar(general_i[:], faults_all[:], 1.0, None, ALU.min).then_inc(path_chosen, 1)
            dve.wait_ge(path_chosen, 1)

            for L in layers:
                n = L.n

                def mark(i, slot):
                    if exists(i, 2):
                        dve.wait_ge(L["z1_ps"], i - 1)
                    V.tensor_copy(loc_now[:, slot, :], edge_loc[:, bass.ds(i * 2, 2)]).then_inc(L["loc_made"], 1)
                    dve.wait_ge(L["loc_made"], i + 1)
                    for h in range(HALVES):
                        last = V.tensor_scalar(onehot[:, slot, h, :], node_iota[:].rearrange("p t q -> p (t q)"),
                                               loc_now[:, slot, h:h + 1], first_slot[:], ALU.is_equal, ALU.max)
                    last.then_inc(L["onehot_made"], 1)

                def messages(i, slot):
                    dve.wait_ge(L["mout_ps"], i + 1)
                    V.tensor_copy(msg_out[:, slot, :, :].rearrange("p s c -> p (s c)"),
                                  ps_e[:, 2 * C:4 * C]).then_inc(L["mout_made"], 1)

                def square_sums(i, slot):
                    for s in range(HALVES):
                        dve.wait_ge(L["z_read"][s], i + 1)
                    for t in range(HALVES * TILES):
                        last = V.tensor_tensor_reduce(squares[:, slot, t, :], z_relu[:, slot, t, :], z_relu[:, slot, t, :], 1.0, 0.0,
                                                      ALU.mult, ALU.add, sumsq[:, slot, t:t + 1])
                    last.then_inc(L["sums_made"], 1)
                    dve.wait_ge(L["sums_made"], i + 1)
                    V.tensor_scalar(sumsq_min[:, slot, :], sumsq[:, slot, :], NORM_EPS ** 2, None,
                                    ALU.max).then_inc(L["sums_min"], 1)

                def residual(i, slot, s):
                    dve.wait_ge(L["z_ps"][s], i + 1)
                    if s == 0:
                        dve.wait_ge(L["res_loaded"][slot], slot_loads(i, slot))
                        if exists(i, 2):
                            dve.wait_ge(L["stored"][slot], slot_loads(i, slot) - 16)
                    V.tensor_tensor(y_out[:, slot, s * TILES:(s + 1) * TILES, :].rearrange("p t c -> p (t c)"),
                                    ps_z[0:PN, s, 0:TILES * C], res_in[:, slot, s, :], ALU.add).then_inc(L["z_read"][s], 1)
                    dve.wait_ge(L["z_read"][s], i + 1)
                    for t in range(s * TILES, (s + 1) * TILES):
                        last = V.bn_stats(stats[:, slot, t, :], y_out[:, slot, t, :])
                    if s == 1:
                        last.then_inc(L["sums_made"], 1)

                def variances(i, slot):
                    dve.wait_ge(L["sums_made"], i + 1)
                    dve.sem_inc(L["sums_begun"], 1)
                    for t in range(HALVES * TILES):
                        last = V.bn_aggr(meanvar[:, slot, t, :], stats[:, slot, t, :])
                    last.then_inc(L["rinv_made"], 1)
                    dve.wait_ge(L["rinv_made"], 2 * i + 1)
                    V.tensor_scalar(sumsq_min[:, slot, :], meanvar[:, slot, :, 1], LN_EPS, None,
                                    ALU.add).then_inc(L["sums_min"], 1)

                def normalise(i, slot):
                    dve.wait_ge(L["root_made"], i + 1)
                    V.reciprocal(rinv[:, slot, :], root[:, slot, :]).then_inc(L["rinv_made"], 1)
                    if n == 0:
                        if exists(i, 2):
                            dve.wait_ge(L["stored"][slot], slot_loads(i, slot) - 16)
                        dve.wait_ge(L["rinv_made"], i + 1)
                        V.tensor_tensor(y_out[:, slot, :, :], z_relu[:, slot, :, :],
                                        rinv[:, slot, :].unsqueeze(2).to_broadcast([PN, HALVES * TILES, C]),
                                        ALU.mult).then_inc(L["out_made"], 1)
                    else:
                        dve.wait_ge(L["rinv_made"], 2 * i + 2)
                        for t in range(HALVES * TILES):
                            last = V.tensor_scalar(y_out[:, slot, t, :], y_out[:, slot, t, :], meanvar[:, slot, t, 0:1],
                                                   rinv[:, slot, t:t + 1], ALU.subtract, ALU.mult)
                        last.then_inc(L["out_made"], 1)

                def step(i, slot):
                    mark(i + 1, 1 - slot)
                    if exists(i, 1):
                        normalise(i - 1, 1 - slot)
                    if n == 1:
                        residual(i, slot, 0)
                    messages(i + 1, 1 - slot)
                    if n == 0:
                        square_sums(i, slot)
                    else:
                        residual(i, slot, 1)
                        variances(i, slot)

                mark(0, 0)
                messages(0, 0)
                over_steps(dve, step)
                normalise(LAST - 1, 1)
                if n == 0:
                    square_sums(LAST, 0)
                else:
                    residual(LAST, 0, 0)
                    residual(LAST, 0, 1)
                    variances(LAST, 0)
                normalise(LAST, 0)

            with dve.If(takes_general_path(dve)):
                for G in general:
                    n = G.n
                    with dve.Fori(0, ERWS) as r:
                        at = [0]

                        def link_edge(ins):
                            at[0] += 1
                            ins.then_inc(G["g_dve"], 1)
                            dve.wait_ge(G["g_dve"], r * 7 + at[0])

                        dve.wait_ge(G["g_edges_loaded"], r * 48 + 48)
                        link_edge(V.tensor_copy(e_dst[:], e_dst_i[:]))
                        link_edge(V.tensor_copy(e_row[:], e_row_i[:]))
                        link_edge(V.tensor_scalar(e_same[:], e_row[:], e_dst[:, 0:1], None, ALU.is_equal))
                        link_edge(V.tensor_tensor(e_earlier[:], e_same[:], before[0:ROW, 0:ROW], ALU.mult))
                        link_edge(V.tensor_reduce(e_count[:], e_earlier[:], mybir.AxisListType.X, ALU.max))
                        link_edge(V.tensor_scalar(e_skip[:], e_count[:], float(N), None, ALU.mult))
                        link_edge(V.tensor_tensor(e_put_i[:], e_skip[:], e_dst[:], ALU.add))
                        dve.wait_ge(G["g_mout"], r + 1)
                        V.tensor_copy(e_out[:], ps_u[0:ROW, 0, 0:C]).then_inc(G["g_mout_made"], 1)
                        dve.wait_ge(G["g_sum"], r + 1)
                        dve.wait_ge(G["g_acc_gathered"], r * 16 + 16)
                        V.tensor_tensor(e_new[:], ps_z[0:ROW, 0, 0:C], e_acc[:], ALU.add).then_inc(G["g_sum_made"], 1)
                    T = HALVES * TILES
                    flat = "p s (t c) -> p (s t) c"
                    for i in over_nodes(dve):
                        at = [0]

                        def link_node(ins):
                            at[0] += 1
                            ins.then_inc(G["g_node_dve"], 1)
                            dve.wait_ge(G["g_node_dve"], i * (3 + n) + at[0])

                        dve.wait_ge(G["g_acc_loaded"], i * 32 + 32)
                        z = x_in[:, 0, :, :].rearrange(flat, t=TILES)
                        y = y_out[:, 0, :, :]
                        if n == 0:
                            link_node(V.tensor_scalar(z_relu[:, 0, :, :], z, 0.0, None, ALU.max))
                            for t in range(T):
                                last = V.tensor_tensor_reduce(squares[:, 0, t, :], z_relu[:, 0, t, :], z_relu[:, 0, t, :],
                                                              1.0, 0.0, ALU.mult, ALU.add, sumsq[:, 0, t:t + 1])
                            link_node(last)
                            V.tensor_scalar(sumsq_min[:, 0, :], sumsq[:, 0, :], NORM_EPS ** 2, None,
                                            ALU.max).then_inc(G["g_sums_made"], 1)
                        else:
                            link_node(V.tensor_tensor(z_relu[:, 0, :, :], z, res_in[:, 0, :, :].rearrange(flat, t=TILES),
                                                      ALU.add))
                            for t in range(T):
                                last = V.bn_stats(stats[:, 0, t, :], z_relu[:, 0, t, :])
                            link_node(last)
                            dve.sem_inc(G["g_begun"], 1)
                            for t in range(T):
                                last = V.bn_aggr(meanvar[:, 0, t, :], stats[:, 0, t, :])
                            link_node(last)
                            V.tensor_scalar(sumsq_min[:, 0, :], meanvar[:, 0, :, 1], LN_EPS, None,
                                            ALU.add).then_inc(G["g_sums_made"], 1)
                        dve.wait_ge(G["g_root_made"], i + 1)
                        link_node(V.reciprocal(rinv[:, 0, :], root[:, 0, :]))
                        for t in range(T):
                            if n == 0:
                                last = V.tensor_scalar(y[:, t, :], z_relu[:, 0, t, :], rinv[:, 0, t:t + 1], None, ALU.mult)
                            else:
                                last = V.tensor_scalar(y[:, t, :], z_relu[:, 0, t, :], meanvar[:, 0, t, 0:1],
                                                       rinv[:, 0, t:t + 1], ALU.subtract, ALU.mult)
                        last.then_inc(G["g_out_made"], 1)


_W = ("wa", "ba", "g", "be", "rm", "rv", "wb", "bb")
_NAMES = [{"wa": f"L0_gnn_w{n}a", "ba": f"L0_gnn_b{n}a", "g": f"L0_gnn_g{n}", "be": f"L0_gnn_be{n}",
           "rm": f"L0_gnn_rm{n}", "rv": f"L0_gnn_rv{n}", "wb": f"L0_gnn_w{n}b", "bb": f"L0_gnn_b{n}b"} for n in (1, 2)]
_INS = ["x", "src", "dst"] + [d[k] for d in _NAMES for k in _W]


def kernel(**inputs):
    import numpy as _np
    import concourse.bacc as _bacc
    from concourse import mybir as _mybir
    from concourse.bass_utils import run_bass_kernel_spmd as _run

    nc = _bacc.Bacc("TRN2", target_bir_lowering=False, num_devices=1)
    arrays, aps = {}, {}
    for name in _INS:
        a = _np.ascontiguousarray(inputs[name])
        arrays[f"in_{name}_dram"] = a
        aps[name] = nc.dram_tensor(f"in_{name}_dram", a.shape, _mybir.dt.from_np(a.dtype), kind="ExternalInput").ap()
    out = nc.dram_tensor("out_dram", inputs["x"].shape, _mybir.dt.float32, kind="ExternalOutput").ap()
    gnn_kernel(nc, aps["x"], aps["src"], aps["dst"], [{k: aps[d[k]] for k in _W} for d in _NAMES], out)
    r = _run(nc, [arrays], core_ids=[0])
    return r.results[0]["out_dram"]
```

```python
from contextlib import ExitStack

import concourse.bass as bass
from concourse import mybir

ALU = mybir.AluOpType
ACT = mybir.ActivationFunctionType
F32 = mybir.dt.float32
BF16 = mybir.dt.bfloat16
F16 = mybir.dt.float16
F32R = mybir.dt.float32r
I32 = mybir.dt.int32

BN_EPS = 1e-5
LN_EPS = 1e-5
NORM_EPS = 1e-12

PN = 112
TILES = 3
SUB = PN * TILES
HALVES = 2
STEP = SUB * HALVES
SLOTS = 128
ROW = 125
WROWS = 5
WIN = ROW * WROWS


class Layer:

    def __init__(self, n, sems):
        self.n = n
        self.sems = sems

    def __getitem__(self, name):
        return self.sems[name]


def exists(i, back):
    return not isinstance(i, int) or i >= back


def gnn_kernel(nc, x, src, dst, weights, out):
    N, C = x.shape
    E = src.shape[0]
    ERWS = E // ROW
    STEPS = -(-N // STEP)
    NSUB = STEPS * HALVES
    SETS = -(-NSUB // 128)
    LAST = STEPS - 1
    assert E % ROW == 0 and C == 128 and STEPS % 2 == 1 and SUB + SLOTS + 1 <= WIN - ROW
    OVERLAP = STEPS * STEP - N
    assert OVERLAP % 2 == 0

    def node0(i):
        return N - STEP if isinstance(i, int) and i == LAST else i * STEP

    def rows_of(t, i):
        return t[bass.ds(node0(i), STEP), :].rearrange("(s p t) c -> p s (t c)", s=HALVES, t=TILES)

    acc_dram = nc.dram_tensor("acc_dram", (N, C), F32, kind="Internal").ap()
    P8, W8 = ERWS // 8, 8 * ROW
    assert N % P8 == 0
    h_dram = nc.dram_tensor("h_dram", (N, C), F32, kind="Internal").ap()
    src_rows = src.rearrange("(r e) -> r e", e=ROW)
    dst_rows = dst.rearrange("(r e) -> r e", e=ROW)

    with ExitStack() as ctx:
        def sb(name, shape, dt=F32):
            return ctx.enter_context(nc.sbuf_tensor(name, shape, dt))

        def sem(name):
            return ctx.enter_context(nc.semaphore(name))

        ident = sb("ident", [128, 128])
        ones_bf = sb("ones_bf", [128, 128], BF16)
        diff_iota = sb("diff_iota", [128, 128])
        node_iota = sb("node_iota", [128, TILES, PN], F16)
        wa_raw = sb("wa_raw", [128, 2, 2 * C])
        wb_raw = sb("wb_raw", [128, 2, C])
        wl_t = sb("wl_t", [128, 2, C])
        wr_t = sb("wr_t", [128, 2, C])
        wd_t = sb("wd_t", [128, 2, C])
        wl_part = sb("wl_part", [128, 2, 2, C], F32R)
        wb_t = sb("wb_t", [128, 2, C])
        wp = sb("wp", [128, 2, C])
        cols = sb("cols", [128, 2, 5])
        bn_s = sb("bn_s", [128, 2])
        bn_t = sb("bn_t", [128, 2])
        bn_u = sb("bn_u", [128, 2])
        bb_row = sb("bb_row", [1, 2, C])
        v_row = sb("v_row", [1, 2, C])
        v_part = sb("v_part", [1, 3, 2, C], BF16)
        v_rest = sb("v_rest", [1, 2, 2, C])
        v_rows = sb("v_rows", [128, 2, C], BF16)
        row_first_i = sb("row_first_i", [128, 8], I32)
        row_first = sb("row_first", [128, 8])
        base_row = sb("base_row", [128, 128 * SETS])
        base_gap = sb("base_gap", [128, 128 * SETS])
        base_col = sb("base_col", [128, SETS])
        base_cgap = sb("base_cgap", [128, SETS])
        below = sb("below", [128, 8, 128 * SETS], BF16)
        win_row = sb("win_row", [128, SETS])
        win_idx = sb("win_idx", [128, SETS, WROWS], I32)
        win_src_i = sb("win_src_i", [128, SETS, WIN], I32)
        win_dst_i = sb("win_dst_i", [128, SETS, WIN], I32)
        win_src = sb("win_src", [128, SETS, WIN])
        win_dst = sb("win_dst", [128, SETS, WIN])
        win_a = sb("win_a", [128, SETS, WIN])
        win_b = sb("win_b", [128, SETS, WIN])
        packed = sb("packed", [128, SETS, WIN - 1], I32)
        found = sb("found", [128, SETS, 1 + SLOTS])
        found_i = sb("found_i", [128, 2, SETS, SLOTS], I32)
        found_f = sb("found_f", [128, 3, SETS, SLOTS])
        edge_idx = sb("edge_idx", [128, NSUB // 2, 4], I32)
        edge_loc = sb("edge_loc", [128, 128 * SETS])
        x_in = sb("x_in", [PN, 2, HALVES, TILES * C])
        res_in = sb("res_in", [PN, 2, HALVES, TILES * C])
        idx_now = sb("idx_now", [128, 2, 4], I32)
        loc_now = sb("loc_now", [128, 2, HALVES])
        gathered = sb("gathered", [128, 2, 4, C])
        x_part = sb("x_part", [128, 2, 2, STEP], F32R)
        g_t = sb("g_t", [128, 2, 4 * SLOTS])
        act_t = sb("act_t", [128, 2, STEP])
        msg_t = sb("msg_t", [128, 2, HALVES * SLOTS])
        msg_part = sb("msg_part", [128, 2, 3, HALVES * C], BF16)
        msg_rest = sb("msg_rest", [128, 2, HALVES * C])
        onehot = sb("onehot", [128, 2, HALVES, SUB], BF16)
        z_relu = sb("z_relu", [PN, 2, HALVES * TILES, C])
        squares = sb("squares", [PN, 2, HALVES * TILES, C])
        sumsq = sb("sumsq", [PN, 2, HALVES * TILES])
        sumsq_min = sb("sumsq_min", [PN, 2, HALVES * TILES])
        root = sb("root", [PN, 2, HALVES * TILES])
        rinv = sb("rinv", [PN, 2, HALVES * TILES])
        y_sum = sb("y_sum", [PN, 2, HALVES * TILES, C])
        y_out = sb("y_out", [PN, 2, HALVES * TILES, C])
        stats = sb("stats", [PN, 2, HALVES * TILES, 6])
        meanvar = sb("meanvar", [PN, 2, HALVES * TILES, 2])
        shift = sb("shift", [PN, 2, HALVES * TILES])
        all_src_i = sb("all_src_i", [P8, W8], I32)
        all_dst_i = sb("all_dst_i", [P8, W8], I32)
        all_next_i = sb("all_next_i", [P8, W8], I32)
        all_src = sb("all_src", [P8, W8])
        all_dst = sb("all_dst", [P8, W8])
        all_next = sb("all_next", [P8, W8])
        all_flag = sb("all_flag", [P8, W8])
        faults = sb("faults", [128, 2 + SETS])
        faults_sum = sb("faults_sum", [1, 2 + SETS])
        faults_all = sb("faults_all", [1, 1])
        general_i = sb("general_i", [1, 1], I32)
        ones_f = sb("ones_f", [128, 1])
        zeros = sb("zeros", [PN, HALVES, TILES * C])
        before = sb("before", [128, 128])
        e_src_i = sb("e_src_i", [ROW, 1], I32)
        e_dst_i = sb("e_dst_i", [ROW, 1], I32)
        e_row_i = sb("e_row_i", [ROW, ROW], I32)
        e_dst = sb("e_dst", [ROW, 1])
        e_row = sb("e_row", [ROW, ROW])
        e_same = sb("e_same", [ROW, ROW])
        e_earlier = sb("e_earlier", [ROW, ROW])
        e_count = sb("e_count", [ROW, 1])
        e_skip = sb("e_skip", [ROW, 1])
        e_put = sb("e_put", [ROW, 1])
        e_put_i = sb("e_put_i", [ROW, 1], I32)
        e_rows = sb("e_rows", [ROW, 2, C])
        e_rows_t = sb("e_rows_t", [128, 2, 128])
        e_msg_t = sb("e_msg_t", [128, 128])
        e_out = sb("e_out", [ROW, C])
        e_acc = sb("e_acc", [ROW, C])
        e_new = sb("e_new", [ROW, C])
        ps_x = ctx.enter_context(nc.psum_tensor("ps_x", [128, HALVES, 512], F32))
        ps_u = ctx.enter_context(nc.psum_tensor("ps_u", [128, HALVES, 512], F32))
        ps_z = ctx.enter_context(nc.psum_tensor("ps_z", [128, HALVES, 512], F32))
        ps_g = ctx.enter_context(nc.psum_tensor("ps_g", [128, 512], F32))
        ps_e = ctx.enter_context(nc.psum_tensor("ps_e", [128, 512], F32))

        weights_loaded = sem("weights_loaded")
        first_loaded = sem("first_loaded")
        consts_made = sem("consts_made")
        dve_setup = sem("dve_setup")
        act_setup = sem("act_setup")
        w_turned = sem("w_turned")
        v_made = sem("v_made")
        v_split = sem("v_split")
        v_moved = sem("v_moved")
        rows_below = sem("rows_below")
        rows_counted = sem("rows_counted")
        win_idx_made = sem("win_idx_made")
        win_loaded = [sem(f"win_loaded{s}") for s in range(SETS)]
        found_made = sem("found_made")
        found_turned = sem("found_turned")
        index_made = sem("index_made")
        next_cleared = sem("next_cleared")
        all_loaded = sem("all_loaded")
        faults_counted = sem("faults_counted")
        faults_summed = sem("faults_summed")
        path_chosen = sem("path_chosen")

        def layer(n):
            L = Layer(n, {what: sem(f"{what}_{n}") for what in (
                    "idx_staged", "gathers_begun",
                    "xt_ps", "gt_ps", "u_ps", "pre_ps", "mout_ps", "z0_ps", "z1_ps",
                    "xl_made", "loc_made", "onehot_made", "mout_made",
                    "mrest_made", "mmid_made", "stats_made", "sums_begun", "sums_min", "var_made",
                    "root_inverted", "rinv_made", "z0_added", "z1_added",
                    "out_begun", "out_made",
                    "xh_made", "mh_made", "gt_made", "act_made", "msg_made", "z0_relued", "z1_relued", "root_made")})
            L.sems["x_loaded"] = [sem(f"x_loaded_{n}_{s}") for s in range(2)]
            L.sems["res_loaded"] = [sem(f"res_loaded_{n}_{s}") for s in range(2)]
            L.sems["rows_gathered"] = [sem(f"rows_gathered_{n}_{s}") for s in range(2)]
            L.sems["stored"] = [sem(f"stored_{n}_{s}") for s in range(2)]
            L.sems["z_read"] = (L["z0_relued"], L["z1_relued"]) if n == 0 else (L["z0_added"], L["z1_added"])
            L.sems["z_ps"] = (L["z0_ps"], L["z1_ps"])
            return L

        layers = [layer(0), layer(1)]
        IN = (x, h_dram)
        OUT = (h_dram, out)

        def general_layer(n):
            return Layer(n, {what: sem(f"{what}_{n}") for what in (
                "g_cleared", "g_begun", "g_ended", "g_edges_loaded", "g_rows_gathered", "g_acc_gathered", "g_scattered",
                "g_turned", "g_turned_made", "g_pre", "g_msg_made", "g_mout", "g_mout_made", "g_sum",
                "g_sum_made", "g_dve", "g_acc_loaded", "g_node_dve", "g_sums_made", "g_root_made",
                "g_out_made", "g_stored")})

        general = [general_layer(0), general_layer(1)]

        def takes_general_path(eng):
            eng.wait_ge(layers[1]["stored"][0], loads(LAST))
            eng.wait_ge(layers[1]["stored"][1], loads(LAST - 1))
            eng.wait_ge(path_chosen, 1)
            return eng.value_load(general_i[0:1, 0:1], min_val=0, max_val=1)

        def loads(i):
            return (i // 2 + 1) * 16

        def slot_loads(i, slot):
            return loads(i) if isinstance(i, int) else (i - slot) * 8 + 16

        def over_steps(eng, step):
            step(0, 0)
            step(1, 1)
            with eng.Fori(2, LAST - 1, 2) as i:
                step(i, 0)
                step(i + 1, 1)

        def over_nodes(eng):
            with eng.Fori(0, LAST) as i:
                yield i
            yield LAST

        block = ctx.enter_context(nc.Block())

        @block.sync
        def _(sp):
            sp.dma_start(row_first_i[0:ERWS // 8, :],
                         dst.rearrange("(p c e) -> p c e", c=8, e=ROW)[:, :, 0],
                         allow_slow_non_contiguous=True).then_inc(first_loaded, 16)
            sp.wait_ge(next_cleared, 1)
            sp.dma_start(all_src_i[:], src.rearrange("(p w) -> p w", w=W8)).then_inc(all_loaded, 16)
            sp.dma_start(all_dst_i[:], dst.rearrange("(p w) -> p w", w=W8)).then_inc(all_loaded, 16)
            sp.dma_start(all_next_i[0:P8 - 1, :], dst[1:E - W8 + 1].rearrange("(p w) -> p w", w=W8)).then_inc(all_loaded, 16)
            sp.dma_start(all_next_i[P8 - 1:P8, 0:W8 - 1],
                         dst[E - W8 + 1:E].rearrange("(p w) -> p w", p=1)).then_inc(all_loaded, 16)
            for n, w in enumerate(weights):
                sp.dma_start(wa_raw[:, n, :], w["wa"]).then_inc(weights_loaded, 16)
                sp.dma_start(wb_raw[:, n, :], w["wb"]).then_inc(weights_loaded, 16)
                sp.dma_start(bb_row[0:1, n, :], w["bb"].rearrange("(a c) -> a c", a=1)).then_inc(weights_loaded, 16)
                for k, name in enumerate(("ba", "g", "be", "rm", "rv")):
                    sp.dma_start(cols[:, n, k:k + 1], w[name].rearrange("(c a) -> c a", a=1),
                                 allow_slow_non_contiguous=True).then_inc(weights_loaded, 16)
            sp.wait_ge(v_split, 1)
            for k in range(3):
                sp.dma_start(v_rows[k:k + 1, :, :], v_part[0:1, k, :, :]).then_inc(v_moved, 16)

            for L in layers:
                if L.n == 1:
                    sp.wait_ge(layers[0]["stored"][0], loads(LAST))
                    sp.wait_ge(layers[0]["stored"][1], loads(LAST - 1))

                def load(i, slot):
                    if exists(i, 2):
                        sp.wait_ge(L["xt_ps"], i - 1)
                    sp.dma_start(x_in[:, slot, :, :], rows_of(IN[L.n], i)).then_inc(L["x_loaded"][slot], 16)

                def load_residual(i, slot):
                    if exists(i, 2):
                        sp.wait_ge(L["z1_added"], i - 1)
                    sp.dma_start(res_in[:, slot, :, :], rows_of(x, i)).then_inc(L["res_loaded"][slot], 16)

                def store(i, slot):
                    sp.wait_ge(L["out_made"], i + 1)
                    if isinstance(i, int) and i == LAST:
                        sp.wait_ge(L["stored"][1], loads(LAST - 1))
                    sp.dma_start(rows_of(OUT[L.n], i),
                                 y_out[:, slot, :, :].rearrange("p (s t) c -> p s (t c)", s=HALVES)
                                 ).then_inc(L["stored"][slot], 16)

                def step(i, slot):
                    load(i, slot)
                    if L.n == 1 and exists(i, 1):
                        load_residual(i - 1, 1 - slot)
                    if exists(i, 4):
                        store(i - 4, slot)

                step(0, 0)
                step(1, 1)
                step(2, 0)
                step(3, 1)
                with sp.Fori(4, LAST - 1, 2) as i:
                    step(i, 0)
                    step(i + 1, 1)
                step(LAST, 0)
                store(LAST - 3, 1)
                if L.n == 1:
                    load_residual(LAST, 0)
                for i in (LAST - 2, LAST - 1, LAST):
                    store(i, i % 2)

            with sp.If(takes_general_path(sp)):
                for G in general:
                    if G.n == 1:
                        sp.wait_ge(general[0]["g_stored"], 16 * STEPS)
                    for i in over_nodes(sp):
                        sp.dma_start(rows_of(acc_dram, i), zeros[:]).then_inc(G["g_cleared"], 16)
                        sp.wait_ge(G["g_cleared"], i * 16 + 16)
                        sp.sem_inc(G["g_ended"], 1)
                    with sp.Fori(0, ERWS) as r:
                        def edges(t, p):
                            return t[bass.ds(r, 1), :].rearrange("r e -> e r" if p == 1 else "r e -> r e")
                        sp.dma_start(e_src_i[:], edges(src_rows, 1), allow_slow_non_contiguous=True
                                     ).then_inc(G["g_edges_loaded"], 16)
                        sp.dma_start(e_dst_i[:], edges(dst_rows, 1), allow_slow_non_contiguous=True
                                     ).then_inc(G["g_edges_loaded"], 16)
                        sp.dma_start(e_row_i[:], edges(dst_rows, 0).to_broadcast([ROW, ROW])
                                     ).then_inc(G["g_edges_loaded"], 16)
                        sp.wait_ge(G["g_scattered"], r * 16 + 16)
                        sp.sem_inc(G["g_ended"], 1)
                    for i in over_nodes(sp):
                        sp.dma_start(x_in[:, 0, :, :], rows_of(acc_dram, i)).then_inc(G["g_acc_loaded"], 16)
                        sp.dma_start(res_in[:, 0, :, :], rows_of(x, i)).then_inc(G["g_acc_loaded"], 16)
                        sp.wait_ge(G["g_out_made"], i + 1)
                        sp.dma_start(rows_of(OUT[G.n], i),
                                     y_out[:, 0, :, :].rearrange("p (s t) c -> p s (t c)", s=HALVES)
                                     ).then_inc(G["g_stored"], 16)
                        sp.wait_ge(G["g_stored"], i * 16 + 16)
                        sp.sem_inc(G["g_ended"], 1)

        @block.gpsimd
        def _(pool):
            nc.gpsimd.iota(diff_iota[:], [[1, 128]], base=0, channel_multiplier=-1,
                           allow_small_or_imprecise_dtypes=True)
            nc.gpsimd.iota(base_row[:], [[SUB, 128 * SETS]], base=0, channel_multiplier=0,
                           allow_small_or_imprecise_dtypes=True)
            for s in range(SETS):
                nc.gpsimd.iota(base_col[:, s:s + 1], [[0, 1]], base=SUB * 128 * s, channel_multiplier=SUB,
                               allow_small_or_imprecise_dtypes=True)
            nc.gpsimd.iota(node_iota[:], [[1, TILES], [TILES, PN]], base=0, channel_multiplier=0,
                           allow_small_or_imprecise_dtypes=True).then_inc(consts_made, 1)
            pool.wait_ge(consts_made, 1)
            nc.gpsimd.memset(node_iota[0:1, :, :], -1.0).then_inc(consts_made, 1)

            pool.wait_ge(win_idx_made, 1)
            for s in range(SETS):
                for r in range(WROWS):
                    for rows, win in ((src_rows, win_src_i), (dst_rows, win_dst_i)):
                        nc.gpsimd.indirect_dma_start(
                            out=win[:, s, r * ROW:(r + 1) * ROW], out_offset=None, in_=rows,
                            in_offset=bass.IndirectOffsetOnAxis(ap=win_idx[:, s, r:r + 1], axis=0),
                        ).then_inc(win_loaded[s], 16)

            pool.wait_ge(index_made, 3)
            for L in layers:
                if L.n == 1:
                    pool.wait_ge(layers[0]["stored"][0], loads(LAST))
                    pool.wait_ge(layers[0]["stored"][1], loads(LAST - 1))

                def gather(i, slot):
                    if exists(i, 2):
                        pool.wait_ge(L["rows_gathered"][slot], slot_loads(i, slot) * 4 - 64)
                    nc.gpsimd.tensor_copy(idx_now[:, slot, :], edge_idx[:, bass.ds(i, 1), :].rearrange(
                        "p i k -> p (i k)")).then_inc(L["idx_staged"], 1)
                    if exists(i, 2):
                        pool.wait_ge(L["gt_ps"], i - 1)
                    pool.wait_ge(L["idx_staged"], i + 1)
                    pool.sem_inc(L["gathers_begun"], 1)
                    for k in range(4):
                        nc.gpsimd.indirect_dma_start(
                            out=gathered[:, slot, k, :], out_offset=None, in_=IN[L.n],
                            in_offset=bass.IndirectOffsetOnAxis(ap=idx_now[:, slot, k:k + 1], axis=0),
                        ).then_inc(L["rows_gathered"][slot], 16)

                over_steps(pool, gather)
                gather(LAST, 0)

            with pool.If(takes_general_path(pool)):
                for G in general:
                    pool.wait_ge(G["g_cleared"], 16 * STEPS)
                    with pool.Fori(0, ERWS) as r:
                        pool.wait_ge(G["g_edges_loaded"], r * 48 + 48)
                        pool.sem_inc(G["g_begun"], 1)
                        for k, idx in enumerate((e_src_i, e_dst_i)):
                            nc.gpsimd.indirect_dma_start(
                                out=e_rows[:, k, :], out_offset=None, in_=IN[G.n],
                                in_offset=bass.IndirectOffsetOnAxis(ap=idx[:, 0:1], axis=0),
                            ).then_inc(G["g_rows_gathered"], 16)
                        nc.gpsimd.indirect_dma_start(
                            out=e_acc[:], out_offset=None, in_=acc_dram,
                            in_offset=bass.IndirectOffsetOnAxis(ap=e_dst_i[:, 0:1], axis=0),
                        ).then_inc(G["g_acc_gathered"], 16)
                        pool.wait_ge(G["g_sum_made"], r + 1)
                        pool.sem_inc(G["g_begun"], 1)
                        nc.gpsimd.indirect_dma_start(
                            out=acc_dram, out_offset=bass.IndirectOffsetOnAxis(ap=e_put_i[:, 0:1], axis=0),
                            in_=e_new[:], in_offset=None, bounds_check=N - 1, oob_is_err=False,
                        ).then_inc(G["g_scattered"], 16)
                        pool.wait_ge(G["g_scattered"], r * 16 + 16)

        @block.tensor
        def _(pe):
            pe.wait_ge(weights_loaded, 16 * 16)
            pe.wait_ge(dve_setup, 1)
            for n in range(2):
                for k, w in enumerate((wa_raw[:, n, 0:C], wa_raw[:, n, C:2 * C], wb_raw[:, n, :])):
                    last = nc.tensor.transpose(ps_x[:, n, k * C:(k + 1) * C], w, ident[:])
            last.then_inc(w_turned, 1)
            pe.wait_ge(rows_below, 1)
            for s in range(SETS):
                for c in range(8):
                    last = nc.tensor.matmul(ps_g[:, s:s + 1], below[0:ERWS // 8, c, s * 128:(s + 1) * 128],
                                            ones_bf[0:ERWS // 8, 0:1], start=(c == 0), stop=(c == 7))
            last.then_inc(rows_counted, 1)
            pe.wait_ge(v_made, 1)
            for n in range(2):
                last = nc.tensor.matmul(ps_u[0:1, n, 0:C], bn_t[:, n:n + 1], wb_t[:, n, :], start=True, stop=True)
            last.then_inc(v_made, 1)
            pe.wait_ge(found_made, 1)
            for k, ps in enumerate((ps_x[:, 0, :], ps_x[:, 1, :], ps_g)):
                for s in range(SETS):
                    last = nc.tensor.transpose(ps[:, s * 128:(s + 1) * 128], found_f[:, k, s, :], ident[:])
            last.then_inc(found_turned, 1)
            pe.wait_ge(faults_counted, 1)
            nc.tensor.matmul(ps_e[0:1, 0:2 + SETS], ones_f[:], faults[:], start=True, stop=True).then_inc(faults_summed, 1)
            pe.wait_ge(path_chosen, 1)
            pe.wait_ge(v_moved, 48)
            pe.wait_ge(index_made, 3)

            for L in layers:
                n = L.n

                def turn(i, slot):
                    pe.wait_ge(L["x_loaded"][slot], slot_loads(i, slot))
                    for s in range(HALVES):
                        for t in range(TILES):
                            last = nc.tensor.transpose(ps_x[:, s, t * PN:(t + 1) * PN],
                                                       x_in[:, slot, s, t * C:(t + 1) * C], ident[0:PN, 0:PN])
                    last.then_inc(L["xt_ps"], 1)
                    pe.wait_ge(L["rows_gathered"][slot], slot_loads(i, slot) * 4)
                    for k in range(4):
                        last = nc.tensor.transpose(ps_g[:, k * SLOTS:(k + 1) * SLOTS], gathered[:, slot, k, :], ident[:])
                    last.then_inc(L["gt_ps"], 1)

                def first_products(i, slot):
                    pe.wait_ge(L["gt_made"], i + 1)
                    pre = ps_e[:, 0:HALVES * SLOTS]
                    nc.tensor.matmul(pre, wr_t[:, n, :], g_t[:, slot, 0:2 * SLOTS], start=True, stop=False)
                    nc.tensor.matmul(pre, wd_t[:, n, :], g_t[:, slot, 2 * SLOTS:], start=False,
                                     stop=True).then_inc(L["pre_ps"], 1)
                    pe.wait_ge(L["xh_made"], i + 1)
                    pe.wait_ge(L["xl_made"], i + 1)
                    for w, k in ((0, 0), (0, 1), (1, 0)):
                        for s in range(HALVES):
                            last = nc.tensor.matmul(ps_u[:, s, 0:SUB], wl_part[:, n, w, :],
                                                    x_part[:, slot, k, s * SUB:(s + 1) * SUB],
                                                    start=(w + k == 0), stop=(w == 1))
                    last.then_inc(L["u_ps"], 1)

                def message_products(i, slot):
                    pe.wait_ge(L["msg_made"], i + 1)
                    for s in range(HALVES):
                        o = ps_e[:, (2 + s) * C:(3 + s) * C]
                        nc.tensor.matmul(o, msg_t[:, slot, s * SLOTS:(s + 1) * SLOTS], wp[:, n, :], start=True, stop=False)
                        last = nc.tensor.matmul(o, ones_bf[:], v_rows[:, n, :], start=False, stop=True)
                    last.then_inc(L["mout_ps"], 1)

                def node_products(i, slot, s):
                    if s == 0:
                        pe.wait_ge(L["act_made"], i + 1)
                        pe.wait_ge(L["onehot_made"], i + 1)
                        pe.wait_ge(L["mout_made"], i + 1)
                    if exists(i, 1):
                        pe.wait_ge(L["z_read"][s], i)
                    for t in range(TILES):
                        o = ps_z[0:PN, s, t * C:(t + 1) * C]
                        at = s * SUB + t * PN
                        nc.tensor.matmul(o, act_t[:, slot, at:at + PN], wp[:, n, :], start=True, stop=False)
                        for k in range(3):
                            last = nc.tensor.matmul(o, onehot[:, slot, s, t * PN:(t + 1) * PN],
                                                    msg_part[:, slot, k, s * C:(s + 1) * C],
                                                    start=False, stop=(k == 2))
                    last.then_inc(L["z_ps"][s], 1)

                def step(i, slot):
                    turn(i + 1, 1 - slot)
                    node_products(i, slot, 0)
                    first_products(i + 1, 1 - slot)
                    message_products(i + 1, 1 - slot)
                    node_products(i, slot, 1)

                turn(0, 0)
                first_products(0, 0)
                message_products(0, 0)
                over_steps(pe, step)
                node_products(LAST, 0, 0)
                node_products(LAST, 0, 1)

            with pe.If(takes_general_path(pe)):
                for G in general:
                    n = G.n
                    with pe.Fori(0, ERWS) as r:
                        pe.wait_ge(G["g_rows_gathered"], r * 32 + 32)
                        for k in range(2):
                            last = nc.tensor.transpose(ps_g[:, k * 128:k * 128 + ROW], e_rows[:, k, :], ident[0:ROW, 0:ROW])
                        last.then_inc(G["g_turned"], 1)
                        pe.wait_ge(G["g_turned_made"], r + 1)
                        nc.tensor.matmul(ps_e[:, 0:ROW], wr_t[:, n, :], e_rows_t[:, 0, 0:ROW], start=True, stop=False)
                        nc.tensor.matmul(ps_e[:, 0:ROW], wd_t[:, n, :], e_rows_t[:, 1, 0:ROW], start=False,
                                         stop=True).then_inc(G["g_pre"], 1)
                        pe.wait_ge(G["g_msg_made"], r + 1)
                        nc.tensor.matmul(ps_u[0:ROW, 0, 0:C], e_msg_t[:, 0:ROW], wp[:, n, :], start=True, stop=False)
                        nc.tensor.matmul(ps_u[0:ROW, 0, 0:C], ones_bf[:, 0:ROW], v_rows[:, n, :], start=False,
                                         stop=True).then_inc(G["g_mout"], 1)
                        pe.wait_ge(G["g_mout_made"], r + 1)
                        nc.tensor.matmul(ps_z[0:ROW, 0, 0:C], e_same[:], e_out[:], start=True,
                                         stop=True).then_inc(G["g_sum"], 1)

        @block.scalar
        def _(act):
            act.wait_ge(act_setup, 1)
            nc.scalar.activation(bn_t[:], bn_u[:], ACT.Sqrt).then_inc(act_setup, 1)

            for L in layers:
                n = L.n
                bias = cols[:, n, 0:1]

                def turn(i, slot):
                    act.wait_ge(L["xt_ps"], i + 1)
                    nc.scalar.activation(x_part[:, slot, 0, :].rearrange("p (s c) -> p s c", s=HALVES),
                                         ps_x[:, :, 0:SUB], ACT.Copy).then_inc(L["xh_made"], 1)
                    act.wait_ge(L["gt_ps"], i + 1)
                    nc.scalar.activation(g_t[:, slot, :], ps_g[:], ACT.Copy).then_inc(L["gt_made"], 1)

                def relu_messages(i, slot):
                    act.wait_ge(L["pre_ps"], i + 1)
                    nc.scalar.activation(msg_t[:, slot, :].rearrange("p (s e) -> p s e", s=HALVES)[:, :, 1:],
                                         ps_e[:, 0:HALVES * SLOTS].rearrange("p (s e) -> p s e", s=HALVES)[:, :, 1:],
                                         ACT.Relu, bias=bias).then_inc(L["msg_made"], 1)

                def relu_nodes(i, slot):
                    act.wait_ge(L["mout_ps"], i + 1)
                    nc.scalar.activation(msg_part[:, slot, 0, :], ps_e[:, 2 * C:4 * C], ACT.Copy).then_inc(L["mh_made"], 1)
                    act.wait_ge(L["u_ps"], i + 1)
                    nc.scalar.activation(act_t[:, slot, :].rearrange("p (s c) -> p s c", s=HALVES), ps_u[:, :, 0:SUB],
                                         ACT.Relu, bias=bias).then_inc(L["act_made"], 1)

                def relu_out(i, slot, s):
                    act.wait_ge(L["z_ps"][s], i + 1)
                    if exists(i, 2) and s == 0:
                        act.wait_ge(L["out_made"], i - 1)
                    nc.scalar.activation(z_relu[:, slot, s * TILES:(s + 1) * TILES, :].rearrange("p t c -> p (t c)"),
                                         ps_z[0:PN, s, 0:TILES * C], ACT.Relu).then_inc(L["z_read"][s], 1)

                def root_of(i, slot):
                    act.wait_ge(L["sums_min"], i + 1)
                    nc.scalar.activation(root[:, slot, :], sumsq_min[:, slot, :], ACT.Sqrt).then_inc(L["root_made"], 1)

                def normalise(i, slot, s):
                    if s == 0:
                        act.wait_ge(L["rinv_made"], i + 1)
                        if exists(i, 2):
                            act.wait_ge(L["stored"][slot], slot_loads(i, slot) - 16)
                    for t in range(s * TILES, (s + 1) * TILES):
                        last = nc.scalar.activation(y_out[:, slot, t, :], y_sum[:, slot, t, :], ACT.Identity,
                                                    bias=shift[:, slot, t:t + 1], scale=rinv[:, slot, t:t + 1])
                    last.then_inc(L["out_begun" if s == 0 else "out_made"], 1)

                def step(i, slot):
                    turn(i + 1, 1 - slot)
                    if n == 0:
                        if exists(i, 1):
                            root_of(i - 1, 1 - slot)
                        relu_out(i, slot, 0)
                    elif exists(i, 2):
                        normalise(i - 2, slot, 1)
                    if n == 1 and exists(i, 1):
                        root_of(i - 1, 1 - slot)
                    relu_messages(i + 1, 1 - slot)
                    relu_nodes(i + 1, 1 - slot)
                    if n == 0:
                        relu_out(i, slot, 1)
                    elif exists(i, 1):
                        normalise(i - 1, 1 - slot, 0)

                turn(0, 0)
                relu_messages(0, 0)
                relu_nodes(0, 0)
                over_steps(act, step)
                if n == 0:
                    root_of(LAST - 1, 1)
                    relu_out(LAST, 0, 0)
                    relu_out(LAST, 0, 1)
                    root_of(LAST, 0)
                else:
                    normalise(LAST - 2, 0, 1)
                    root_of(LAST - 1, 1)
                    normalise(LAST - 1, 1, 0)
                    normalise(LAST - 1, 1, 1)
                    root_of(LAST, 0)
                    normalise(LAST, 0, 0)
                    normalise(LAST, 0, 1)

            with act.If(takes_general_path(act)):
                for G in general:
                    with act.Fori(0, ERWS) as r:
                        act.wait_ge(G["g_turned"], r + 1)
                        nc.scalar.activation(e_rows_t[:, :, 0:ROW], ps_g[:, 0:256].rearrange(
                            "p (k e) -> p k e", k=2)[:, :, 0:ROW], ACT.Copy).then_inc(G["g_turned_made"], 1)
                        act.wait_ge(G["g_pre"], r + 1)
                        nc.scalar.activation(e_msg_t[:, 0:ROW], ps_e[:, 0:ROW], ACT.Relu,
                                             bias=cols[:, G.n, 0:1]).then_inc(G["g_msg_made"], 1)
                    for i in over_nodes(act):
                        act.wait_ge(G["g_sums_made"], i + 1)
                        nc.scalar.activation(root[:, 0, :], sumsq_min[:, 0, :], ACT.Sqrt).then_inc(G["g_root_made"], 1)

        @block.vector
        def _(dve):
            done = [0]

            def link(ins):
                done[0] += 1
                ins.then_inc(dve_setup, 1)
                dve.wait_ge(dve_setup, done[0])

            V = nc.vector
            dve.wait_ge(consts_made, 2)
            V.memset(all_next_i[:], N).then_inc(next_cleared, 1)
            V.memset(ones_bf[:], 1.0)
            V.memset(ones_f[:], 1.0)
            V.memset(zeros[:], 0.0)
            V.memset(found[:, :, 0:1], 0.0)
            V.memset(msg_t[:], 0.0)
            V.memset(faults[:], 0.0)
            V.tensor_scalar(before[:], diff_iota[:], 0.0, None, ALU.is_lt)
            V.memset(v_rows[:], 0.0)
            link(V.tensor_scalar(ident[:], diff_iota[:], 0.0, None, ALU.is_equal))
            for v, gap in ((base_row, base_gap), (base_col, base_cgap)):
                link(V.tensor_scalar(gap[:], v[:], float(LAST * STEP), -float(OVERLAP), ALU.is_ge, ALU.mult))
                link(V.tensor_tensor(gap[:], gap[:], v[:], ALU.add))
                link(V.tensor_scalar(v[:], gap[:], float(N - SUB), None, ALU.min))
            dve.wait_ge(first_loaded, 16)
            q = ERWS // 8
            link(V.tensor_copy(row_first[0:q, :], row_first_i[0:q, :]))
            for c in range(8):
                last = V.tensor_scalar(below[0:q, c, :], base_row[0:q, :], row_first[0:q, c:c + 1], None, ALU.is_gt)
            last.then_inc(rows_below, 1)
            dve.wait_ge(rows_counted, 1)
            link(V.tensor_scalar(win_row[:], ps_g[:, 0:SETS], 1.0, 0.0, ALU.subtract, ALU.max))
            link(V.tensor_scalar(win_row[:], win_row[:], float(ERWS - WROWS), None, ALU.min))
            for r in range(WROWS):
                last = V.tensor_scalar(win_idx[:, :, r], win_row[:], float(r), None, ALU.add)
            last.then_inc(win_idx_made, 1)

            dve.wait_ge(all_loaded, 64)
            V.tensor_copy(all_src[:], all_src_i[:])
            V.tensor_copy(all_dst[:], all_dst_i[:])
            link(V.tensor_copy(all_next[:], all_next_i[:]))
            V.tensor_tensor(all_src[:], all_src[:], all_dst[:], ALU.is_equal)
            link(V.tensor_tensor(all_next[:], all_next[:], all_dst[:], ALU.subtract))
            link(V.tensor_scalar(all_dst[:], all_next[:], 0.0, None, ALU.is_gt))
            V.tensor_tensor_reduce(all_flag[:], all_src[:], all_dst[:], 1.0, 0.0, ALU.mult, ALU.add, faults[0:P8, 1:2])
            link(V.tensor_scalar(all_next[:], all_next[:], 0.0, None, ALU.is_lt))
            V.tensor_reduce(faults[0:P8, 0:1], all_next[:], mybir.AxisListType.X, ALU.add)
            link(V.tensor_scalar(faults[0:P8, 1:2], faults[0:P8, 1:2], float(N // P8), None, ALU.subtract))

            dve.wait_ge(weights_loaded, 16 * 16)
            V.tensor_scalar(bn_u[:], cols[:, :, 4], BN_EPS, None, ALU.add).then_inc(act_setup, 1)
            dve.wait_ge(w_turned, 1)
            for n in range(2):
                for k, w in enumerate((wl_t, wr_t, wb_t)):
                    last = V.tensor_copy(w[:, n, :], ps_x[:, n, k * C:(k + 1) * C])
            link(last)
            link(V.tensor_copy(wl_part[:, :, 0, :], wl_t[:]))
            V.tensor_tensor(wl_part[:, :, 1, :], wl_t[:], wl_part[:, :, 0, :].bitcast(F32), ALU.subtract)
            dve.wait_ge(act_setup, 2)
            link(V.reciprocal(bn_u[:], bn_t[:]))
            link(V.tensor_tensor(bn_s[:], bn_u[:], cols[:, :, 1], ALU.mult))
            link(V.tensor_tensor(bn_u[:], bn_s[:], cols[:, :, 3], ALU.mult))
            V.tensor_tensor(bn_t[:], cols[:, :, 2], bn_u[:], ALU.subtract).then_inc(v_made, 1)
            for n in range(2):
                V.tensor_tensor(wd_t[:, n, :], wl_t[:, n, :], wr_t[:, n, :], ALU.subtract)
                V.tensor_scalar(wp[:, n, :], wb_t[:, n, :], bn_s[:, n:n + 1], None, ALU.mult)
            dve.wait_ge(v_made, 2)
            link(V.tensor_tensor(v_row[:], ps_u[0:1, :, 0:C], bb_row[:], ALU.add))
            link(V.tensor_copy(v_part[0:1, 0], v_row[:]))
            link(V.tensor_tensor(v_rest[0:1, 0], v_row[:], v_part[0:1, 0], ALU.subtract))
            link(V.tensor_copy(v_part[0:1, 1], v_rest[0:1, 0]))
            link(V.tensor_tensor(v_rest[0:1, 1], v_rest[0:1, 0], v_part[0:1, 1], ALU.subtract))
            V.tensor_copy(v_part[0:1, 2], v_rest[0:1, 1]).then_inc(v_split, 1)

            M = WIN - 1
            for s in range(SETS):
                dve.wait_ge(win_loaded[s], 2 * WROWS * 16)
                V.tensor_copy(win_src[:, s, :], win_src_i[:, s, :])
                link(V.tensor_copy(win_dst[:, s, :], win_dst_i[:, s, :]))
                link(V.tensor_tensor(win_a[:, s, 0:M], win_dst[:, s, 0:M], win_dst[:, s, 1:], ALU.not_equal))
                link(V.tensor_tensor(win_b[:, s, 0:M], win_dst[:, s, 0:M], win_src[:, s, 0:M], ALU.is_equal))
                link(V.tensor_tensor(win_b[:, s, 0:M], win_a[:, s, 0:M], win_b[:, s, 0:M], ALU.mult))
                link(V.tensor_scalar(win_a[:, s, 0:M], win_b[:, s, 0:M], -1.0, 1.0, ALU.mult, ALU.add))
                link(V.tensor_scalar(win_dst[:, s, 0:M], win_dst[:, s, 0:M], base_col[:, s:s + 1], None, ALU.subtract))
                link(V.scalar_tensor_tensor(win_b[:, s, 0:M], win_dst[:, s, 0:M], 0.0, win_a[:, s, 0:M],
                                            ALU.is_ge, ALU.mult))
                link(V.scalar_tensor_tensor(win_a[:, s, 0:M], win_dst[:, s, 0:M], float(SUB), win_b[:, s, 0:M],
                                            ALU.is_lt, ALU.mult))
                V.scalar_tensor_tensor(win_dst_i[:, s, 0:M], win_dst[:, s, 0:M], 2049.0, win_a[:, s, 0:M],
                                       ALU.add, ALU.mult)
                link(V.tensor_tensor(win_src_i[:, s, 0:M], win_src[:, s, 0:M], win_a[:, s, 0:M], ALU.mult))
                link(V.scalar_tensor_tensor(packed[:, s, :], win_dst_i[:, s, 0:M], 17, win_src_i[:, s, 0:M],
                                            ALU.logical_shift_left, ALU.bitwise_or))
            start = done[0]
            for r in range(SLOTS // 8):
                for s in range(SETS):
                    if r:
                        dve.wait_ge(dve_setup, start + (2 * r - 1) * SETS + s + 1)
                    V.max(found[:, s, 8 * r + 1:8 * r + 9], packed[:, s, :].bitcast(F32)).then_inc(dve_setup, 1)
                for s in range(SETS):
                    dve.wait_ge(dve_setup, start + 2 * r * SETS + s + 1)
                    V.match_replace(packed[:, s, :].bitcast(F32), found[:, s, 8 * r + 1:8 * r + 9],
                                    packed[:, s, :].bitcast(F32), 0.0).then_inc(dve_setup, 1)
            done[0] = start + 2 * SETS * SLOTS // 8
            dve.wait_ge(dve_setup, done[0])
            for s in range(SETS):
                last = V.tensor_reduce(faults[:, 2 + s:3 + s], packed[:, s, :].bitcast(F32), mybir.AxisListType.X, ALU.max)
            link(last)
            V.tensor_tensor(faults[:, 2:], faults[:, 2:], found[:, :, SLOTS], ALU.max)
            bits = found[:, :, 0:SLOTS].bitcast(I32)
            V.tensor_scalar(found_i[:, 0], bits, (1 << 17) - 1, None, ALU.bitwise_and)
            link(V.tensor_scalar(found_i[:, 1], bits, 17, 2047, ALU.logical_shift_right, ALU.bitwise_and))
            V.tensor_copy(found_f[:, 0], found_i[:, 0])
            link(V.tensor_scalar(found_f[:, 1], found_i[:, 1], 1.0, None, ALU.subtract))
            for s in range(SETS):
                last = V.tensor_scalar(found_f[:, 2, s, :], found_f[:, 1, s, :], 0.0, base_col[:, s:s + 1],
                                       ALU.max, ALU.add)
            last.then_inc(found_made, 1)
            V.tensor_scalar(faults[:, 2:], faults[:, 2:], 0.0, None, ALU.is_gt).then_inc(faults_counted, 1)
            dve.wait_ge(found_turned, 1)
            V.tensor_copy(edge_idx[:, :, 0:2], ps_x[:, 0, 0:NSUB].rearrange("p (i h) -> p i h", h=2)).then_inc(index_made, 1)
            V.tensor_copy(edge_idx[:, :, 2:4], ps_g[:, 0:NSUB].rearrange("p (i h) -> p i h", h=2)).then_inc(index_made, 1)
            V.tensor_copy(edge_loc[:, 0:NSUB], ps_x[:, 1, 0:NSUB]).then_inc(index_made, 1)
            dve.wait_ge(index_made, 3)
            dve.wait_ge(faults_summed, 1)
            link(V.tensor_copy(faults_sum[:], ps_e[0:1, 0:2 + SETS]))
            link(V.tensor_tensor(faults_sum[:], faults_sum[:], faults_sum[:], ALU.mult))
            link(V.tensor_reduce(faults_all[:], faults_sum[:], mybir.AxisListType.X, ALU.max))
            V.tensor_scalar(general_i[:], faults_all[:], 1.0, None, ALU.min).then_inc(path_chosen, 1)
            dve.wait_ge(path_chosen, 1)

            for L in layers:
                n = L.n

                def mark(i, slot):
                    if exists(i, 2):
                        dve.wait_ge(L["z1_ps"], i - 1)
                    V.tensor_copy(loc_now[:, slot, :], edge_loc[:, bass.ds(i * 2, 2)]).then_inc(L["loc_made"], 1)
                    dve.wait_ge(L["loc_made"], i + 1)
                    for h in range(HALVES):
                        last = V.tensor_scalar(onehot[:, slot, h, :], node_iota[:].rearrange("p t q -> p (t q)"),
                                               loc_now[:, slot, h:h + 1], None, ALU.is_equal)
                    last.then_inc(L["onehot_made"], 1)

                def turn(i, slot):
                    dve.wait_ge(L["xh_made"], i + 1)
                    V.tensor_tensor(x_part[:, slot, 1, :].rearrange("p (s c) -> p s c", s=HALVES), ps_x[:, :, 0:SUB],
                                    x_part[:, slot, 0, :].bitcast(F32).rearrange("p (s c) -> p s c", s=HALVES),
                                    ALU.subtract).then_inc(L["xl_made"], 1)

                def messages(i, slot):
                    dve.wait_ge(L["mh_made"], i + 1)
                    V.tensor_tensor(msg_rest[:, slot, :], ps_e[:, 2 * C:4 * C], msg_part[:, slot, 0, :],
                                    ALU.subtract).then_inc(L["mrest_made"], 1)
                    dve.wait_ge(L["mrest_made"], i + 1)
                    V.tensor_copy(msg_part[:, slot, 1, :], msg_rest[:, slot, :]).then_inc(L["mmid_made"], 1)
                    dve.wait_ge(L["mmid_made"], i + 1)
                    V.tensor_tensor(msg_part[:, slot, 2, :], msg_rest[:, slot, :], msg_part[:, slot, 1, :],
                                    ALU.subtract).then_inc(L["mout_made"], 1)

                def square_sums(i, slot, s):
                    dve.wait_ge(L["z_read"][s], i + 1)
                    for t in range(s * TILES, (s + 1) * TILES):
                        last = V.tensor_tensor_reduce(squares[:, slot, t, :], z_relu[:, slot, t, :], z_relu[:, slot, t, :],
                                                      1.0, 0.0, ALU.mult, ALU.add, sumsq[:, slot, t:t + 1])
                    if s == 1:
                        last.then_inc(L["stats_made"], 1)

                def floor(i, slot):
                    dve.wait_ge(L["stats_made"], i + 1)
                    V.tensor_scalar(sumsq_min[:, slot, :], sumsq[:, slot, :], NORM_EPS ** 2, None,
                                    ALU.max).then_inc(L["sums_min"], 1)

                def residual(i, slot, s):
                    dve.wait_ge(L["z_ps"][s], i + 1)
                    if s == 0:
                        dve.wait_ge(L["res_loaded"][slot], slot_loads(i, slot))
                    if exists(i, 2):
                        dve.wait_ge(L["out_begun" if s == 0 else "out_made"], i - 1)
                    V.tensor_tensor(y_sum[:, slot, s * TILES:(s + 1) * TILES, :].rearrange("p t c -> p (t c)"),
                                    ps_z[0:PN, s, 0:TILES * C], res_in[:, slot, s, :], ALU.add).then_inc(L["z_read"][s], 1)
                    dve.wait_ge(L["z_read"][s], i + 1)
                    for t in range(s * TILES, (s + 1) * TILES):
                        last = V.bn_stats(stats[:, slot, t, :], y_sum[:, slot, t, :])
                    if s == 1:
                        last.then_inc(L["stats_made"], 1)

                def variances(i, slot):
                    dve.wait_ge(L["stats_made"], i + 1)
                    dve.sem_inc(L["sums_begun"], 1)
                    for t in range(HALVES * TILES):
                        last = V.bn_aggr(meanvar[:, slot, t, :], stats[:, slot, t, :])
                    last.then_inc(L["var_made"], 1)
                    dve.wait_ge(L["var_made"], i + 1)
                    V.tensor_scalar(sumsq_min[:, slot, :], meanvar[:, slot, :, 1], LN_EPS, None,
                                    ALU.add).then_inc(L["sums_min"], 1)

                def inverse_root(i, slot):
                    dve.wait_ge(L["root_made"], i + 1)
                    V.reciprocal(rinv[:, slot, :], root[:, slot, :]).then_inc(L["root_inverted"], 1)

                def normalise(i, slot):
                    if exists(i, 2):
                        dve.wait_ge(L["stored"][slot], slot_loads(i, slot) - 16)
                    dve.wait_ge(L["root_inverted"], i + 1)
                    V.tensor_tensor(y_out[:, slot, :, :], z_relu[:, slot, :, :],
                                    rinv[:, slot, :].unsqueeze(2).to_broadcast([PN, HALVES * TILES, C]),
                                    ALU.mult).then_inc(L["out_made"], 1)

                def shift_of(i, slot):
                    dve.wait_ge(L["root_inverted"], i + 1)
                    V.scalar_tensor_tensor(shift[:, slot, :], meanvar[:, slot, :, 0], -1.0, rinv[:, slot, :],
                                           ALU.mult, ALU.mult).then_inc(L["rinv_made"], 1)

                def step(i, slot):
                    if exists(i, 1):
                        if n == 0:
                            square_sums(i - 1, 1 - slot, 1)
                            floor(i - 1, 1 - slot)
                        else:
                            residual(i - 1, 1 - slot, 1)
                    turn(i + 1, 1 - slot)
                    if n == 0:
                        if exists(i, 1):
                            inverse_root(i - 1, 1 - slot)
                        mark(i + 1, 1 - slot)
                        if exists(i, 1):
                            normalise(i - 1, 1 - slot)
                        square_sums(i, slot, 0)
                        messages(i + 1, 1 - slot)
                    else:
                        if exists(i, 1):
                            variances(i - 1, 1 - slot)
                        residual(i, slot, 0)
                        if exists(i, 1):
                            inverse_root(i - 1, 1 - slot)
                        mark(i + 1, 1 - slot)
                        if exists(i, 1):
                            shift_of(i - 1, 1 - slot)
                        messages(i + 1, 1 - slot)

                turn(0, 0)
                mark(0, 0)
                messages(0, 0)
                over_steps(dve, step)
                if n == 0:
                    square_sums(LAST - 1, 1, 1)
                    floor(LAST - 1, 1)
                    inverse_root(LAST - 1, 1)
                    normalise(LAST - 1, 1)
                    square_sums(LAST, 0, 0)
                    square_sums(LAST, 0, 1)
                    floor(LAST, 0)
                    inverse_root(LAST, 0)
                    normalise(LAST, 0)
                else:
                    residual(LAST - 1, 1, 1)
                    residual(LAST, 0, 0)
                    variances(LAST - 1, 1)
                    inverse_root(LAST - 1, 1)
                    shift_of(LAST - 1, 1)
                    residual(LAST, 0, 1)
                    variances(LAST, 0)
                    inverse_root(LAST, 0)
                    shift_of(LAST, 0)

            with dve.If(takes_general_path(dve)):
                for G in general:
                    n = G.n
                    with dve.Fori(0, ERWS) as r:
                        at = [0]

                        def link_edge(ins):
                            at[0] += 1
                            ins.then_inc(G["g_dve"], 1)
                            dve.wait_ge(G["g_dve"], r * 7 + at[0])

                        dve.wait_ge(G["g_edges_loaded"], r * 48 + 48)
                        link_edge(V.tensor_copy(e_dst[:], e_dst_i[:]))
                        link_edge(V.tensor_copy(e_row[:], e_row_i[:]))
                        link_edge(V.tensor_scalar(e_same[:], e_row[:], e_dst[:, 0:1], None, ALU.is_equal))
                        link_edge(V.tensor_tensor(e_earlier[:], e_same[:], before[0:ROW, 0:ROW], ALU.mult))
                        link_edge(V.tensor_reduce(e_count[:], e_earlier[:], mybir.AxisListType.X, ALU.max))
                        link_edge(V.tensor_scalar(e_skip[:], e_count[:], float(N), None, ALU.mult))
                        link_edge(V.tensor_tensor(e_put_i[:], e_skip[:], e_dst[:], ALU.add))
                        dve.wait_ge(G["g_mout"], r + 1)
                        V.tensor_copy(e_out[:], ps_u[0:ROW, 0, 0:C]).then_inc(G["g_mout_made"], 1)
                        dve.wait_ge(G["g_sum"], r + 1)
                        dve.wait_ge(G["g_acc_gathered"], r * 16 + 16)
                        V.tensor_tensor(e_new[:], ps_z[0:ROW, 0, 0:C], e_acc[:], ALU.add).then_inc(G["g_sum_made"], 1)
                    T = HALVES * TILES
                    flat = "p s (t c) -> p (s t) c"
                    for i in over_nodes(dve):
                        at = [0]

                        def link_node(ins):
                            at[0] += 1
                            ins.then_inc(G["g_node_dve"], 1)
                            dve.wait_ge(G["g_node_dve"], i * (3 + n) + at[0])

                        dve.wait_ge(G["g_acc_loaded"], i * 32 + 32)
                        z = x_in[:, 0, :, :].rearrange(flat, t=TILES)
                        y = y_out[:, 0, :, :]
                        if n == 0:
                            link_node(V.tensor_scalar(z_relu[:, 0, :, :], z, 0.0, None, ALU.max))
                            for t in range(T):
                                last = V.tensor_tensor_reduce(squares[:, 0, t, :], z_relu[:, 0, t, :], z_relu[:, 0, t, :],
                                                              1.0, 0.0, ALU.mult, ALU.add, sumsq[:, 0, t:t + 1])
                            link_node(last)
                            V.tensor_scalar(sumsq_min[:, 0, :], sumsq[:, 0, :], NORM_EPS ** 2, None,
                                            ALU.max).then_inc(G["g_sums_made"], 1)
                        else:
                            link_node(V.tensor_tensor(z_relu[:, 0, :, :], z, res_in[:, 0, :, :].rearrange(flat, t=TILES),
                                                      ALU.add))
                            for t in range(T):
                                last = V.bn_stats(stats[:, 0, t, :], z_relu[:, 0, t, :])
                            link_node(last)
                            dve.sem_inc(G["g_begun"], 1)
                            for t in range(T):
                                last = V.bn_aggr(meanvar[:, 0, t, :], stats[:, 0, t, :])
                            link_node(last)
                            V.tensor_scalar(sumsq_min[:, 0, :], meanvar[:, 0, :, 1], LN_EPS, None,
                                            ALU.add).then_inc(G["g_sums_made"], 1)
                        dve.wait_ge(G["g_root_made"], i + 1)
                        link_node(V.reciprocal(rinv[:, 0, :], root[:, 0, :]))
                        for t in range(T):
                            if n == 0:
                                last = V.tensor_scalar(y[:, t, :], z_relu[:, 0, t, :], rinv[:, 0, t:t + 1], None, ALU.mult)
                            else:
                                last = V.tensor_scalar(y[:, t, :], z_relu[:, 0, t, :], meanvar[:, 0, t, 0:1],
                                                       rinv[:, 0, t:t + 1], ALU.subtract, ALU.mult)
                        last.then_inc(G["g_out_made"], 1)


_W = ("wa", "ba", "g", "be", "rm", "rv", "wb", "bb")
_NAMES = [{"wa": f"L0_gnn_w{n}a", "ba": f"L0_gnn_b{n}a", "g": f"L0_gnn_g{n}", "be": f"L0_gnn_be{n}",
           "rm": f"L0_gnn_rm{n}", "rv": f"L0_gnn_rv{n}", "wb": f"L0_gnn_w{n}b", "bb": f"L0_gnn_b{n}b"} for n in (1, 2)]
_INS = ["x", "src", "dst"] + [d[k] for d in _NAMES for k in _W]


def kernel(**inputs):
    import numpy as _np
    import concourse.bacc as _bacc
    from concourse import mybir as _mybir
    from concourse.bass_utils import run_bass_kernel_spmd as _run

    nc = _bacc.Bacc("TRN2", target_bir_lowering=False, num_devices=1)
    arrays, aps = {}, {}
    for name in _INS:
        a = _np.ascontiguousarray(inputs[name])
        arrays[f"in_{name}_dram"] = a
        aps[name] = nc.dram_tensor(f"in_{name}_dram", a.shape, _mybir.dt.from_np(a.dtype), kind="ExternalInput").ap()
    out = nc.dram_tensor("out_dram", inputs["x"].shape, _mybir.dt.float32, kind="ExternalOutput").ap()
    gnn_kernel(nc, aps["x"], aps["src"], aps["dst"], [{k: aps[d[k]] for k in _W} for d in _NAMES], out)
    r = _run(nc, [arrays], core_ids=[0])
    return r.results[0]["out_dram"]
```

```python
from contextlib import ExitStack

import concourse.bass as bass
from concourse import mybir

ALU = mybir.AluOpType
ACT = mybir.ActivationFunctionType
F32 = mybir.dt.float32
BF16 = mybir.dt.bfloat16
F16 = mybir.dt.float16
F32R = mybir.dt.float32r
I32 = mybir.dt.int32

BN_EPS = 1e-5
LN_EPS = 1e-5
NORM_EPS = 1e-12

PN = 120
TILES = 3
SUB = PN * TILES
HALVES = 2
STEP = SUB * HALVES
SLOTS = 128
ROW = 125
WROWS = 5
WIN = ROW * WROWS


class Layer:

    def __init__(self, n, sems):
        self.n = n
        self.sems = sems

    def __getitem__(self, name):
        return self.sems[name]


def exists(i, back):
    return not isinstance(i, int) or i >= back


def gnn_kernel(nc, x, src, dst, weights, out):
    N, C = x.shape
    E = src.shape[0]
    ERWS = E // ROW
    STEPS = -(-N // STEP)
    NSUB = STEPS * HALVES
    SETS = -(-NSUB // 128)
    LAST = STEPS - 1
    assert E % ROW == 0 and C == 128 and STEPS % 2 == 1 and SUB + SLOTS <= WIN - ROW
    ROUNDS = SLOTS // 8
    SET_STEPS = 128 // HALVES
    assert SETS == 3 and 4 + 2 * ROUNDS < SET_STEPS
    OVERLAP = STEPS * STEP - N
    assert OVERLAP % 2 == 0

    def node0(i):
        return N - STEP if isinstance(i, int) and i == LAST else i * STEP

    def rows_of(t, i):
        return t[bass.ds(node0(i), STEP), :].rearrange("(s p t) c -> p s (t c)", s=HALVES, t=TILES)

    acc_dram = nc.dram_tensor("acc_dram", (N, C), F32, kind="Internal").ap()
    P8, W8 = ERWS // 8, 8 * ROW
    assert N % P8 == 0
    h_dram = nc.dram_tensor("h_dram", (N, C), F32, kind="Internal").ap()
    src_rows = src.rearrange("(r e) -> r e", e=ROW)
    dst_rows = dst.rearrange("(r e) -> r e", e=ROW)

    with ExitStack() as ctx:
        def sb(name, shape, dt=F32):
            return ctx.enter_context(nc.sbuf_tensor(name, shape, dt))

        def sem(name):
            return ctx.enter_context(nc.semaphore(name))

        ident = sb("ident", [128, 128])
        ones_bf = sb("ones_bf", [128, 128], BF16)
        diff_iota = sb("diff_iota", [128, 128])
        node_iota = sb("node_iota", [128, TILES, PN], F16)
        wa_raw = sb("wa_raw", [128, 2, 2 * C])
        wb_raw = sb("wb_raw", [128, 2, C])
        wl_t = sb("wl_t", [128, 2, C])
        wr_t = sb("wr_t", [128, 2, C])
        wd_t = sb("wd_t", [128, 2, C])
        wl_part = sb("wl_part", [128, 2, 2, C], F32R)
        wb_t = sb("wb_t", [128, 2, C])
        wp = sb("wp", [128, 2, C])
        cols = sb("cols", [128, 2, 5])
        bn_s = sb("bn_s", [128, 2])
        bn_t = sb("bn_t", [128, 2])
        bn_u = sb("bn_u", [128, 2])
        bb_row = sb("bb_row", [1, 2, C])
        v_row = sb("v_row", [1, 2, C])
        v_part = sb("v_part", [1, 3, 2, C], BF16)
        v_rest = sb("v_rest", [1, 2, 2, C])
        v_rows = sb("v_rows", [128, 2, C], BF16)
        row_first_i = sb("row_first_i", [128, 8], I32)
        row_first = sb("row_first", [128, 8])
        base_row = sb("base_row", [128, 128 * SETS])
        base_gap = sb("base_gap", [128, 128 * SETS])
        base_col = sb("base_col", [128, SETS])
        base_cgap = sb("base_cgap", [128, SETS])
        below = sb("below", [128, 8, 128 * SETS], BF16)
        win_row = sb("win_row", [128, SETS])
        win_idx = sb("win_idx", [128, SETS, WROWS], I32)
        win_src_i = sb("win_src_i", [128, SETS, WIN], I32)
        win_dst_i = sb("win_dst_i", [128, SETS, WIN], I32)
        win_src = sb("win_src", [128, SETS, WIN])
        win_dst = sb("win_dst", [128, SETS, WIN])
        win_a = sb("win_a", [128, SETS, WIN])
        win_b = sb("win_b", [128, SETS, WIN])
        packed = sb("packed", [128, SETS, WIN - 1], I32)
        largest = sb("largest", [128, 8])
        found = sb("found", [128, SETS, 1 + SLOTS])
        found_i = sb("found_i", [128, 2, SETS, SLOTS], I32)
        found_f = sb("found_f", [128, 3, SETS, SLOTS])
        edge_idx = sb("edge_idx", [128, NSUB // 2, 4], I32)
        edge_loc = sb("edge_loc", [128, 128 * SETS])
        x_in = sb("x_in", [PN, 2, HALVES, TILES * C])
        res_in = sb("res_in", [PN, 2, HALVES, TILES * C])
        idx_now = sb("idx_now", [128, 2, 4], I32)
        loc_now = sb("loc_now", [128, 2, HALVES])
        gathered = sb("gathered", [128, 2, 4, C])
        x_part = sb("x_part", [128, 2, 2, STEP], F32R)
        g_t = sb("g_t", [128, 2, 4 * SLOTS])
        act_t = sb("act_t", [128, 2, STEP])
        msg_t = sb("msg_t", [128, 2, HALVES * SLOTS])
        msg_part = sb("msg_part", [128, 2, 3, HALVES * C], BF16)
        msg_rest = sb("msg_rest", [128, 2, HALVES * C])
        onehot = sb("onehot", [128, 2, HALVES, SUB], BF16)
        z_relu = sb("z_relu", [PN, 2, HALVES * TILES, C])
        squares = sb("squares", [PN, 2, HALVES * TILES, C])
        sumsq = sb("sumsq", [PN, 2, HALVES * TILES])
        sumsq_min = sb("sumsq_min", [PN, 2, HALVES * TILES])
        root = sb("root", [PN, 2, HALVES * TILES])
        rinv = sb("rinv", [PN, 2, HALVES * TILES])
        y_sum = sb("y_sum", [PN, 2, HALVES * TILES, C])
        y_out = sb("y_out", [PN, 2, HALVES * TILES, C])
        stats = sb("stats", [PN, 2, HALVES * TILES, 6])
        meanvar = sb("meanvar", [PN, 2, HALVES * TILES, 2])
        shift = sb("shift", [PN, 2, HALVES * TILES])
        all_src_i = sb("all_src_i", [P8, W8], I32)
        all_dst_i = sb("all_dst_i", [P8, W8], I32)
        all_next_i = sb("all_next_i", [P8, W8], I32)
        all_src = sb("all_src", [P8, W8])
        all_dst = sb("all_dst", [P8, W8])
        all_next = sb("all_next", [P8, W8])
        all_flag = sb("all_flag", [P8, W8])
        faults = sb("faults", [128, 2 + SETS])
        faults_sum = sb("faults_sum", [1, 2 + SETS])
        faults_all = sb("faults_all", [1, 1])
        general_i = sb("general_i", [1, 1], I32)
        ones_f = sb("ones_f", [128, 1])
        zeros = sb("zeros", [PN, HALVES, TILES * C])
        before = sb("before", [128, 128])
        e_src_i = sb("e_src_i", [ROW, 1], I32)
        e_dst_i = sb("e_dst_i", [ROW, 1], I32)
        e_row_i = sb("e_row_i", [ROW, ROW], I32)
        e_dst = sb("e_dst", [ROW, 1])
        e_row = sb("e_row", [ROW, ROW])
        e_same = sb("e_same", [ROW, ROW])
        e_earlier = sb("e_earlier", [ROW, ROW])
        e_count = sb("e_count", [ROW, 1])
        e_skip = sb("e_skip", [ROW, 1])
        e_put_i = sb("e_put_i", [ROW, 1], I32)
        e_rows = sb("e_rows", [ROW, 2, C])
        e_rows_t = sb("e_rows_t", [128, 2, 128])
        e_msg_t = sb("e_msg_t", [128, 128])
        e_out = sb("e_out", [ROW, C])
        e_acc = sb("e_acc", [ROW, C])
        e_new = sb("e_new", [ROW, C])
        ps_x = ctx.enter_context(nc.psum_tensor("ps_x", [128, HALVES, 512], F32))
        ps_u = ctx.enter_context(nc.psum_tensor("ps_u", [128, HALVES, 512], F32))
        ps_z = ctx.enter_context(nc.psum_tensor("ps_z", [128, HALVES, 512], F32))
        ps_g = ctx.enter_context(nc.psum_tensor("ps_g", [128, 512], F32))
        ps_e = ctx.enter_context(nc.psum_tensor("ps_e", [128, 512], F32))

        weights_loaded = sem("weights_loaded")
        first_loaded = sem("first_loaded")
        consts_made = sem("consts_made")
        dve_setup = sem("dve_setup")
        act_setup = sem("act_setup")
        w_turned = sem("w_turned")
        v_made = sem("v_made")
        v_split = sem("v_split")
        v_moved = sem("v_moved")
        rows_below = sem("rows_below")
        rows_counted = sem("rows_counted")
        win_idx_made = sem("win_idx_made")
        win_loaded = [sem(f"win_loaded{s}") for s in range(SETS)]
        taken = [sem(f"taken{s}") for s in range(SETS)]
        found_made = sem("found_made")
        found_turned = sem("found_turned")
        index_made = sem("index_made")
        next_cleared = sem("next_cleared")
        all_loaded = sem("all_loaded")
        all_as_floats = sem("all_as_floats")
        win_as_floats = sem("win_as_floats")
        faults_counted = sem("faults_counted")
        rounds_begun = sem("rounds_begun")
        path_chosen = sem("path_chosen")

        def layer(n):
            L = Layer(n, {what: sem(f"{what}_{n}") for what in (
                    "idx_staged", "gathers_begun",
                    "xt_ps", "gt_ps", "u_ps", "pre_ps", "mout_ps", "z0_ps", "z1_ps",
                    "xl_made", "loc_made", "onehot_made", "mout_made",
                    "mrest_made", "mmid_made", "stats_made", "sums_begun", "sums_min", "var_made",
                    "root_inverted", "rinv_made", "z0_added", "z1_added",
                    "out_begun", "out_made",
                    "xh_made", "mh_made", "gt_made", "act_made", "msg_made", "z0_relued", "z1_relued", "root_made")})
            L.sems["x_loaded"] = [sem(f"x_loaded_{n}_{s}") for s in range(2)]
            L.sems["res_loaded"] = [sem(f"res_loaded_{n}_{s}") for s in range(2)]
            L.sems["rows_gathered"] = [sem(f"rows_gathered_{n}_{s}") for s in range(2)]
            L.sems["stored"] = [sem(f"stored_{n}_{s}") for s in range(2)]
            L.sems["z_read"] = (L["z0_relued"], L["z1_relued"]) if n == 0 else (L["z0_added"], L["z1_added"])
            L.sems["z_ps"] = (L["z0_ps"], L["z1_ps"])
            return L

        layers = [layer(0), layer(1)]
        IN = (x, h_dram)
        OUT = (h_dram, out)

        def general_layer(n):
            return Layer(n, {what: sem(f"{what}_{n}") for what in (
                "g_cleared", "g_begun", "g_ended", "g_edges_loaded", "g_rows_gathered", "g_acc_gathered", "g_scattered",
                "g_turned", "g_turned_made", "g_pre", "g_msg_made", "g_mout", "g_mout_made", "g_sum",
                "g_sum_made", "g_dve", "g_acc_loaded", "g_node_dve", "g_sums_made", "g_root_made",
                "g_out_made", "g_stored")})

        general = [general_layer(0), general_layer(1)]

        def takes_general_path(eng):
            eng.wait_ge(layers[1]["stored"][0], loads(LAST))
            eng.wait_ge(layers[1]["stored"][1], loads(LAST - 1))
            eng.wait_ge(path_chosen, 1)
            return eng.value_load(general_i[0:1, 0:1], min_val=0, max_val=1)

        def loads(i):
            return (i // 2 + 1) * 16

        def slot_loads(i, slot):
            return loads(i) if isinstance(i, int) else (i - slot) * 8 + 16

        def over_steps(eng, step, first=0, until=LAST, unrolled=2):
            if first == 0:
                step(0, 0)
                step(1, 1)
                first = 2
            assert (until - first) % unrolled == 0
            with eng.Fori(first, until - 1, unrolled) as i:
                for j in range(unrolled):
                    step(i + j, j % 2)

        def found_by(s):
            return 2 + 2 * ROUNDS * s

        def over_nodes(eng):
            with eng.Fori(0, LAST) as i:
                yield i
            yield LAST

        block = ctx.enter_context(nc.Block())

        @block.sync
        def _(sp):
            sp.dma_start(row_first_i[0:ERWS // 8, :],
                         dst.rearrange("(p c e) -> p c e", c=8, e=ROW)[:, :, 0],
                         allow_slow_non_contiguous=True).then_inc(first_loaded, 16)
            for n, w in enumerate(weights):
                sp.dma_start(wa_raw[:, n, :], w["wa"]).then_inc(weights_loaded, 16)
                sp.dma_start(wb_raw[:, n, :], w["wb"]).then_inc(weights_loaded, 16)
                sp.dma_start(bb_row[0:1, n, :], w["bb"].rearrange("(a c) -> a c", a=1)).then_inc(weights_loaded, 16)
                for k, name in enumerate(("ba", "g", "be", "rm", "rv")):
                    sp.dma_start(cols[:, n, k:k + 1], w[name].rearrange("(c a) -> c a", a=1),
                                 allow_slow_non_contiguous=True).then_inc(weights_loaded, 16)
            sp.wait_ge(next_cleared, 1)
            sp.dma_start(all_src_i[:], src.rearrange("(p w) -> p w", w=W8)).then_inc(all_loaded, 16)
            sp.dma_start(all_dst_i[:], dst.rearrange("(p w) -> p w", w=W8)).then_inc(all_loaded, 16)
            sp.dma_start(all_next_i[0:P8 - 1, :], dst[1:E - W8 + 1].rearrange("(p w) -> p w", w=W8)).then_inc(all_loaded, 16)
            sp.dma_start(all_next_i[P8 - 1:P8, 0:W8 - 1],
                         dst[E - W8 + 1:E].rearrange("(p w) -> p w", p=1)).then_inc(all_loaded, 16)
            sp.wait_ge(v_split, 1)
            for k in range(3):
                sp.dma_start(v_rows[k:k + 1, :, :], v_part[0:1, k, :, :]).then_inc(v_moved, 16)

            for L in layers:
                if L.n == 1:
                    sp.wait_ge(layers[0]["stored"][0], loads(LAST))
                    sp.wait_ge(layers[0]["stored"][1], loads(LAST - 1))

                def load(i, slot):
                    if exists(i, 2):
                        sp.wait_ge(L["xt_ps"], i - 1)
                    sp.dma_start(x_in[:, slot, :, :], rows_of(IN[L.n], i)).then_inc(L["x_loaded"][slot], 16)

                def load_residual(i, slot):
                    if exists(i, 2):
                        sp.wait_ge(L["z1_added"], i - 1)
                    sp.dma_start(res_in[:, slot, :, :], rows_of(x, i)).then_inc(L["res_loaded"][slot], 16)

                def store(i, slot):
                    sp.wait_ge(L["out_made"], i + 1)
                    if isinstance(i, int) and i == LAST:
                        sp.wait_ge(L["stored"][1], loads(LAST - 1))
                    sp.dma_start(rows_of(OUT[L.n], i),
                                 y_out[:, slot, :, :].rearrange("p (s t) c -> p s (t c)", s=HALVES)
                                 ).then_inc(L["stored"][slot], 16)

                def step(i, slot):
                    load(i, slot)
                    if L.n == 1 and exists(i, 1):
                        load_residual(i - 1, 1 - slot)
                    if exists(i, 4):
                        store(i - 4, slot)

                step(0, 0)
                step(1, 1)
                step(2, 0)
                step(3, 1)
                with sp.Fori(4, LAST - 1, 2) as i:
                    step(i, 0)
                    step(i + 1, 1)
                step(LAST, 0)
                store(LAST - 3, 1)
                if L.n == 1:
                    load_residual(LAST, 0)
                for i in (LAST - 2, LAST - 1, LAST):
                    store(i, i % 2)

            with sp.If(takes_general_path(sp)):
                for G in general:
                    if G.n == 1:
                        sp.wait_ge(general[0]["g_stored"], 16 * STEPS)
                    for i in over_nodes(sp):
                        sp.dma_start(rows_of(acc_dram, i), zeros[:]).then_inc(G["g_cleared"], 16)
                        sp.wait_ge(G["g_cleared"], i * 16 + 16)
                        sp.sem_inc(G["g_ended"], 1)
                    with sp.Fori(0, ERWS) as r:
                        def edges(t, p):
                            return t[bass.ds(r, 1), :].rearrange("r e -> e r" if p == 1 else "r e -> r e")
                        sp.dma_start(e_src_i[:], edges(src_rows, 1), allow_slow_non_contiguous=True
                                     ).then_inc(G["g_edges_loaded"], 16)
                        sp.dma_start(e_dst_i[:], edges(dst_rows, 1), allow_slow_non_contiguous=True
                                     ).then_inc(G["g_edges_loaded"], 16)
                        sp.dma_start(e_row_i[:], edges(dst_rows, 0).to_broadcast([ROW, ROW])
                                     ).then_inc(G["g_edges_loaded"], 16)
                        sp.wait_ge(G["g_scattered"], r * 16 + 16)
                        sp.sem_inc(G["g_ended"], 1)
                    for i in over_nodes(sp):
                        sp.dma_start(x_in[:, 0, :, :], rows_of(acc_dram, i)).then_inc(G["g_acc_loaded"], 16)
                        sp.dma_start(res_in[:, 0, :, :], rows_of(x, i)).then_inc(G["g_acc_loaded"], 16)
                        sp.wait_ge(G["g_out_made"], i + 1)
                        sp.dma_start(rows_of(OUT[G.n], i),
                                     y_out[:, 0, :, :].rearrange("p (s t) c -> p s (t c)", s=HALVES)
                                     ).then_inc(G["g_stored"], 16)
                        sp.wait_ge(G["g_stored"], i * 16 + 16)
                        sp.sem_inc(G["g_ended"], 1)

        @block.gpsimd
        def _(pool):
            nc.gpsimd.iota(diff_iota[:], [[1, 128]], base=0, channel_multiplier=-1,
                           allow_small_or_imprecise_dtypes=True)
            nc.gpsimd.iota(base_row[:], [[SUB, 128 * SETS]], base=0, channel_multiplier=0,
                           allow_small_or_imprecise_dtypes=True)
            for s in range(SETS):
                nc.gpsimd.iota(base_col[:, s:s + 1], [[0, 1]], base=SUB * 128 * s, channel_multiplier=SUB,
                               allow_small_or_imprecise_dtypes=True)
            nc.gpsimd.iota(node_iota[:], [[1, TILES], [TILES, PN]], base=0, channel_multiplier=0,
                           allow_small_or_imprecise_dtypes=True).then_inc(consts_made, 1)
            pool.wait_ge(consts_made, 1)
            nc.gpsimd.memset(node_iota[0:1, :, :], -1.0).then_inc(consts_made, 1)

            pool.wait_ge(win_idx_made, 1)
            for s in range(SETS):
                for r in range(WROWS):
                    for rows, win in ((src_rows, win_src_i), (dst_rows, win_dst_i)):
                        nc.gpsimd.indirect_dma_start(
                            out=win[:, s, r * ROW:(r + 1) * ROW], out_offset=None, in_=rows,
                            in_offset=bass.IndirectOffsetOnAxis(ap=win_idx[:, s, r:r + 1], axis=0),
                        ).then_inc(win_loaded[s], 16)

            for L in layers:
                if L.n == 1:
                    pool.wait_ge(layers[0]["stored"][0], loads(LAST))
                    pool.wait_ge(layers[0]["stored"][1], loads(LAST - 1))

                def gather(i, slot):
                    if exists(i, 2):
                        pool.wait_ge(L["rows_gathered"][slot], slot_loads(i, slot) * 4 - 64)
                    nc.gpsimd.tensor_copy(idx_now[:, slot, :], edge_idx[:, bass.ds(i, 1), :].rearrange(
                        "p i k -> p (i k)")).then_inc(L["idx_staged"], 1)
                    if exists(i, 2):
                        pool.wait_ge(L["gt_ps"], i - 1)
                    pool.wait_ge(L["idx_staged"], i + 1)
                    pool.sem_inc(L["gathers_begun"], 1)
                    for k in range(4):
                        nc.gpsimd.indirect_dma_start(
                            out=gathered[:, slot, k, :], out_offset=None, in_=IN[L.n],
                            in_offset=bass.IndirectOffsetOnAxis(ap=idx_now[:, slot, k:k + 1], axis=0),
                        ).then_inc(L["rows_gathered"][slot], 16)

                if L.n == 0:
                    for s in range(SETS):
                        pool.wait_ge(index_made, 3 * s + 3)
                        over_steps(pool, gather, SET_STEPS * s, min(SET_STEPS * (s + 1), LAST))
                else:
                    over_steps(pool, gather)
                gather(LAST, 0)

            with pool.If(takes_general_path(pool)):
                for G in general:
                    pool.wait_ge(G["g_cleared"], 16 * STEPS)
                    with pool.Fori(0, ERWS) as r:
                        pool.wait_ge(G["g_edges_loaded"], r * 48 + 48)
                        pool.sem_inc(G["g_begun"], 1)
                        for k, idx in enumerate((e_src_i, e_dst_i)):
                            nc.gpsimd.indirect_dma_start(
                                out=e_rows[:, k, :], out_offset=None, in_=IN[G.n],
                                in_offset=bass.IndirectOffsetOnAxis(ap=idx[:, 0:1], axis=0),
                            ).then_inc(G["g_rows_gathered"], 16)
                        nc.gpsimd.indirect_dma_start(
                            out=e_acc[:], out_offset=None, in_=acc_dram,
                            in_offset=bass.IndirectOffsetOnAxis(ap=e_dst_i[:, 0:1], axis=0),
                        ).then_inc(G["g_acc_gathered"], 16)
                        pool.wait_ge(G["g_sum_made"], r + 1)
                        pool.sem_inc(G["g_begun"], 1)
                        nc.gpsimd.indirect_dma_start(
                            out=acc_dram, out_offset=bass.IndirectOffsetOnAxis(ap=e_put_i[:, 0:1], axis=0),
                            in_=e_new[:], in_offset=None, bounds_check=N - 1, oob_is_err=False,
                        ).then_inc(G["g_scattered"], 16)
                        pool.wait_ge(G["g_scattered"], r * 16 + 16)

        @block.tensor
        def _(pe):
            pe.wait_ge(rows_below, 1)
            for s in range(SETS):
                for c in range(8):
                    last = nc.tensor.matmul(ps_g[:, s:s + 1], below[0:ERWS // 8, c, s * 128:(s + 1) * 128],
                                            ones_bf[0:ERWS // 8, 0:1], start=(c == 0), stop=(c == 7))
            last.then_inc(rows_counted, 1)
            pe.wait_ge(weights_loaded, 16 * 16)
            pe.wait_ge(dve_setup, 1)
            for n in range(2):
                for k, w in enumerate((wa_raw[:, n, 0:C], wa_raw[:, n, C:2 * C], wb_raw[:, n, :])):
                    last = nc.tensor.transpose(ps_x[:, n, k * C:(k + 1) * C], w, ident[:])
            last.then_inc(w_turned, 1)
            pe.wait_ge(v_made, 1)
            for n in range(2):
                last = nc.tensor.matmul(ps_u[0:1, n, 0:C], bn_t[:, n:n + 1], wb_t[:, n, :], start=True, stop=True)
            last.then_inc(v_made, 1)

            def turn_found(s):
                pe.wait_ge(found_made, s + 1)
                for k in range(3):
                    last = nc.tensor.transpose(ps_g[:, k * 128:(k + 1) * 128], found_f[:, k, s, :], ident[:])
                if s == SETS - 1:
                    pe.wait_ge(faults_counted, 1)
                    last = nc.tensor.matmul(ps_g[0:1, 384:386 + SETS], ones_f[:], faults[:], start=True, stop=True)
                last.then_inc(found_turned, 1)
                if s == SETS - 1:
                    pe.wait_ge(path_chosen, 1)
                pe.wait_ge(index_made, 3 * s + 3)

            turn_found(0)
            pe.wait_ge(v_moved, 48)

            for L in layers:
                n = L.n

                def turn(i, slot):
                    pe.wait_ge(L["rows_gathered"][slot], slot_loads(i, slot) * 4)
                    for k in range(4):
                        last = nc.tensor.transpose(ps_g[:, k * SLOTS:(k + 1) * SLOTS], gathered[:, slot, k, :], ident[:])
                    last.then_inc(L["gt_ps"], 1)
                    pe.wait_ge(L["x_loaded"][slot], slot_loads(i, slot))
                    for s in range(HALVES):
                        for t in range(TILES):
                            last = nc.tensor.transpose(ps_x[:, s, t * PN:(t + 1) * PN],
                                                       x_in[:, slot, s, t * C:(t + 1) * C], ident[0:PN, 0:PN])
                    last.then_inc(L["xt_ps"], 1)

                def first_products(i, slot):
                    pe.wait_ge(L["gt_made"], i + 1)
                    pre = ps_e[:, 0:HALVES * SLOTS]
                    nc.tensor.matmul(pre, wr_t[:, n, :], g_t[:, slot, 0:2 * SLOTS], start=True, stop=False)
                    nc.tensor.matmul(pre, wd_t[:, n, :], g_t[:, slot, 2 * SLOTS:], start=False,
                                     stop=True).then_inc(L["pre_ps"], 1)
                    pe.wait_ge(L["xh_made"], i + 1)
                    pe.wait_ge(L["xl_made"], i + 1)
                    for w, k in ((0, 0), (0, 1), (1, 0)):
                        for s in range(HALVES):
                            last = nc.tensor.matmul(ps_u[:, s, 0:SUB], wl_part[:, n, w, :],
                                                    x_part[:, slot, k, s * SUB:(s + 1) * SUB],
                                                    start=(w + k == 0), stop=(w == 1))
                    last.then_inc(L["u_ps"], 1)

                def message_products(i, slot):
                    pe.wait_ge(L["msg_made"], i + 1)
                    nc.tensor.matmul(ps_e[:, 2 * C:4 * C].rearrange("p (s c) -> p s c", s=HALVES), ones_bf[:],
                                     v_rows[:, n:n + 1, :].to_broadcast([128, HALVES, C]), start=True, stop=False)
                    for s in range(HALVES):
                        last = nc.tensor.matmul(ps_e[:, (2 + s) * C:(3 + s) * C], msg_t[:, slot, s * SLOTS:(s + 1) * SLOTS],
                                                wp[:, n, :], start=False, stop=(s == HALVES - 1))
                    last.then_inc(L["mout_ps"], 1)

                def node_products(i, slot, s):
                    if s == 0:
                        pe.wait_ge(L["act_made"], i + 1)
                    if exists(i, 1):
                        pe.wait_ge(L["z_read"][s], i)
                    for t in range(TILES):
                        at = s * SUB + t * PN
                        nc.tensor.matmul(ps_z[0:PN, s, t * C:(t + 1) * C], act_t[:, slot, at:at + PN], wp[:, n, :],
                                         start=(t == 0), stop=False)
                    if s == 0:
                        pe.wait_ge(L["onehot_made"], i * 2 + 2)
                        pe.wait_ge(L["mout_made"], i + 1)
                    for t in range(TILES):
                        for k in range(3):
                            last = nc.tensor.matmul(ps_z[0:PN, s, t * C:(t + 1) * C],
                                                    onehot[:, slot, s, t * PN:(t + 1) * PN],
                                                    msg_part[:, slot, k, s * C:(s + 1) * C],
                                                    start=False, stop=(t == TILES - 1 and k == 2))
                    last.then_inc(L["z_ps"][s], 1)

                def step(i, slot):
                    turn(i + 1, 1 - slot)
                    node_products(i, slot, 0)
                    first_products(i + 1, 1 - slot)
                    message_products(i + 1, 1 - slot)
                    node_products(i, slot, 1)

                turn(0, 0)
                first_products(0, 0)
                message_products(0, 0)
                if n == 0:
                    first = 0
                    for s in range(1, SETS):
                        over_steps(pe, step, first, found_by(s) + 2)
                        turn_found(s)
                        first = found_by(s) + 2
                    over_steps(pe, step, first)
                else:
                    over_steps(pe, step, unrolled=4)
                node_products(LAST, 0, 0)
                node_products(LAST, 0, 1)

            with pe.If(takes_general_path(pe)):
                for G in general:
                    n = G.n
                    with pe.Fori(0, ERWS) as r:
                        pe.wait_ge(G["g_rows_gathered"], r * 32 + 32)
                        for k in range(2):
                            last = nc.tensor.transpose(ps_g[:, k * 128:k * 128 + ROW], e_rows[:, k, :], ident[0:ROW, 0:ROW])
                        last.then_inc(G["g_turned"], 1)
                        pe.wait_ge(G["g_turned_made"], r + 1)
                        nc.tensor.matmul(ps_e[:, 0:ROW], wr_t[:, n, :], e_rows_t[:, 0, 0:ROW], start=True, stop=False)
                        nc.tensor.matmul(ps_e[:, 0:ROW], wd_t[:, n, :], e_rows_t[:, 1, 0:ROW], start=False,
                                         stop=True).then_inc(G["g_pre"], 1)
                        pe.wait_ge(G["g_msg_made"], r + 1)
                        nc.tensor.matmul(ps_u[0:ROW, 0, 0:C], e_msg_t[:, 0:ROW], wp[:, n, :], start=True, stop=False)
                        nc.tensor.matmul(ps_u[0:ROW, 0, 0:C], ones_bf[:, 0:ROW], v_rows[:, n, :], start=False,
                                         stop=True).then_inc(G["g_mout"], 1)
                        pe.wait_ge(G["g_mout_made"], r + 1)
                        nc.tensor.matmul(ps_z[0:ROW, 0, 0:C], e_same[:], e_out[:], start=True,
                                         stop=True).then_inc(G["g_sum"], 1)

        @block.scalar
        def _(act):
            act.wait_ge(act_setup, 1)
            nc.scalar.activation(bn_t[:], bn_u[:], ACT.Sqrt).then_inc(act_setup, 1)
            act.wait_ge(all_loaded, 64)
            for ints, floats in ((all_src_i, all_src), (all_dst_i, all_dst), (all_next_i, all_next)):
                nc.scalar.activation(floats[:], ints[:], ACT.Copy).then_inc(all_as_floats, 1)
            for s in range(SETS):
                act.wait_ge(win_loaded[s], 2 * WROWS * 16)
                for ints, floats in ((win_dst_i, win_dst), (win_src_i, win_src)):
                    nc.scalar.activation(floats[:, s, :], ints[:, s, :], ACT.Copy).then_inc(win_as_floats, 1)

            for L in layers:
                n = L.n
                bias = cols[:, n, 0:1]

                def turn(i, slot):
                    act.wait_ge(L["gt_ps"], i + 1)
                    nc.scalar.activation(g_t[:, slot, :], ps_g[:], ACT.Copy).then_inc(L["gt_made"], 1)
                    act.wait_ge(L["xt_ps"], i + 1)
                    nc.scalar.activation(x_part[:, slot, 0, :].rearrange("p (s c) -> p s c", s=HALVES),
                                         ps_x[:, :, 0:SUB], ACT.Copy).then_inc(L["xh_made"], 1)

                def relu_messages(i, slot):
                    act.wait_ge(L["pre_ps"], i + 1)
                    nc.scalar.activation(msg_t[:, slot, :].rearrange("p (s e) -> p s e", s=HALVES)[:, :, 1:],
                                         ps_e[:, 0:HALVES * SLOTS].rearrange("p (s e) -> p s e", s=HALVES)[:, :, 1:],
                                         ACT.Relu, bias=bias).then_inc(L["msg_made"], 1)

                def relu_nodes(i, slot):
                    act.wait_ge(L["mout_ps"], i + 1)
                    nc.scalar.activation(msg_part[:, slot, 0, :], ps_e[:, 2 * C:4 * C], ACT.Copy).then_inc(L["mh_made"], 1)
                    act.wait_ge(L["u_ps"], i + 1)
                    nc.scalar.activation(act_t[:, slot, :].rearrange("p (s c) -> p s c", s=HALVES), ps_u[:, :, 0:SUB],
                                         ACT.Relu, bias=bias).then_inc(L["act_made"], 1)

                def relu_out(i, slot, s):
                    act.wait_ge(L["z_ps"][s], i + 1)
                    if exists(i, 2) and s == 0:
                        act.wait_ge(L["out_made"], i - 1)
                    nc.scalar.activation(z_relu[:, slot, s * TILES:(s + 1) * TILES, :].rearrange("p t c -> p (t c)"),
                                         ps_z[0:PN, s, 0:TILES * C], ACT.Relu).then_inc(L["z_read"][s], 1)

                def root_of(i, slot):
                    act.wait_ge(L["sums_min"], i + 1)
                    nc.scalar.activation(root[:, slot, :], sumsq_min[:, slot, :], ACT.Sqrt).then_inc(L["root_made"], 1)

                def normalise(i, slot, part):
                    if part == 0:
                        act.wait_ge(L["rinv_made"], i + 1)
                        if exists(i, 2):
                            act.wait_ge(L["stored"][slot], slot_loads(i, slot) - 16)
                    for t in (2 * part, 2 * part + 1):
                        last = nc.scalar.activation(y_out[:, slot, t, :], y_sum[:, slot, t, :], ACT.Identity,
                                                    bias=shift[:, slot, t:t + 1], scale=rinv[:, slot, t:t + 1])
                    if part:
                        last.then_inc(L["out_begun" if part == 1 else "out_made"], 1)

                def step(i, slot):
                    turn(i + 1, 1 - slot)
                    if n == 0:
                        if exists(i, 1):
                            root_of(i - 1, 1 - slot)
                        relu_out(i, slot, 0)
                    elif exists(i, 2):
                        normalise(i - 2, slot, 1)
                    relu_messages(i + 1, 1 - slot)
                    if n == 1 and exists(i, 2):
                        normalise(i - 2, slot, 2)
                    if n == 1 and exists(i, 1):
                        root_of(i - 1, 1 - slot)
                    relu_nodes(i + 1, 1 - slot)
                    if n == 0:
                        relu_out(i, slot, 1)
                    elif exists(i, 1):
                        normalise(i - 1, 1 - slot, 0)

                turn(0, 0)
                relu_messages(0, 0)
                relu_nodes(0, 0)
                over_steps(act, step, unrolled=2 + 2 * n)
                if n == 0:
                    root_of(LAST - 1, 1)
                    relu_out(LAST, 0, 0)
                    relu_out(LAST, 0, 1)
                    root_of(LAST, 0)
                else:
                    for part in (1, 2):
                        normalise(LAST - 2, 0, part)
                    root_of(LAST - 1, 1)
                    for part in range(3):
                        normalise(LAST - 1, 1, part)
                    root_of(LAST, 0)
                    for part in range(3):
                        normalise(LAST, 0, part)

            with act.If(takes_general_path(act)):
                for G in general:
                    with act.Fori(0, ERWS) as r:
                        act.wait_ge(G["g_turned"], r + 1)
                        nc.scalar.activation(e_rows_t[:, :, 0:ROW], ps_g[:, 0:256].rearrange(
                            "p (k e) -> p k e", k=2)[:, :, 0:ROW], ACT.Copy).then_inc(G["g_turned_made"], 1)
                        act.wait_ge(G["g_pre"], r + 1)
                        nc.scalar.activation(e_msg_t[:, 0:ROW], ps_e[:, 0:ROW], ACT.Relu,
                                             bias=cols[:, G.n, 0:1]).then_inc(G["g_msg_made"], 1)
                    for i in over_nodes(act):
                        act.wait_ge(G["g_sums_made"], i + 1)
                        nc.scalar.activation(root[:, 0, :], sumsq_min[:, 0, :], ACT.Sqrt).then_inc(G["g_root_made"], 1)

        @block.vector
        def _(dve):
            done = [0]

            def link(ins):
                done[0] += 1
                ins.then_inc(dve_setup, 1)
                dve.wait_ge(dve_setup, done[0])

            V = nc.vector
            dve.wait_ge(consts_made, 2)
            V.memset(ones_bf[:], 1.0)
            link(V.tensor_scalar(ident[:], diff_iota[:], 0.0, None, ALU.is_equal))
            for v, gap in ((base_row, base_gap), (base_col, base_cgap)):
                link(V.tensor_scalar(gap[:], v[:], float(LAST * STEP), -float(OVERLAP), ALU.is_ge, ALU.mult))
                link(V.tensor_tensor(gap[:], gap[:], v[:], ALU.add))
                link(V.tensor_scalar(v[:], gap[:], float(N - SUB), None, ALU.min))
            dve.wait_ge(first_loaded, 16)
            q = ERWS // 8
            link(V.tensor_copy(row_first[0:q, :], row_first_i[0:q, :]))
            for c in range(8):
                last = V.tensor_scalar(below[0:q, c, :], base_row[0:q, :], row_first[0:q, c:c + 1], None, ALU.is_gt)
            last.then_inc(rows_below, 1)
            V.memset(all_next_i[:], N).then_inc(next_cleared, 1)
            V.memset(ones_f[:], 1.0)
            V.memset(zeros[:], 0.0)
            V.memset(found[:, :, 0:1], 0.0)
            V.memset(msg_t[:], 0.0)
            V.memset(faults[:], 0.0)
            V.tensor_scalar(before[:], diff_iota[:], 0.0, None, ALU.is_lt)
            V.memset(v_rows[:], 0.0)
            dve.wait_ge(rows_counted, 1)
            link(V.tensor_scalar(win_row[:], ps_g[:, 0:SETS], 1.0, 0.0, ALU.subtract, ALU.max))
            link(V.tensor_scalar(win_row[:], win_row[:], float(ERWS - WROWS), None, ALU.min))
            for r in range(WROWS):
                last = V.tensor_scalar(win_idx[:, :, r], win_row[:], float(r), None, ALU.add)
            last.then_inc(win_idx_made, 1)

            dve.wait_ge(weights_loaded, 16 * 16)
            V.tensor_scalar(bn_u[:], cols[:, :, 4], BN_EPS, None, ALU.add).then_inc(act_setup, 1)
            dve.wait_ge(w_turned, 1)
            for n in range(2):
                for k, w in enumerate((wl_t, wr_t, wb_t)):
                    last = V.tensor_copy(w[:, n, :], ps_x[:, n, k * C:(k + 1) * C])
            link(last)
            link(V.tensor_copy(wl_part[:, :, 0, :], wl_t[:]))
            V.tensor_tensor(wl_part[:, :, 1, :], wl_t[:], wl_part[:, :, 0, :].bitcast(F32), ALU.subtract)
            dve.wait_ge(act_setup, 2)
            link(V.reciprocal(bn_u[:], bn_t[:]))
            link(V.tensor_tensor(bn_s[:], bn_u[:], cols[:, :, 1], ALU.mult))
            link(V.tensor_tensor(bn_u[:], bn_s[:], cols[:, :, 3], ALU.mult))
            V.tensor_tensor(bn_t[:], cols[:, :, 2], bn_u[:], ALU.subtract).then_inc(v_made, 1)
            for n in range(2):
                V.tensor_tensor(wd_t[:, n, :], wl_t[:, n, :], wr_t[:, n, :], ALU.subtract)
                V.tensor_scalar(wp[:, n, :], wb_t[:, n, :], bn_s[:, n:n + 1], None, ALU.mult)
            dve.wait_ge(v_made, 2)
            link(V.tensor_tensor(v_row[:], ps_u[0:1, :, 0:C], bb_row[:], ALU.add))
            link(V.tensor_copy(v_part[0:1, 0], v_row[:]))
            link(V.tensor_tensor(v_rest[0:1, 0], v_row[:], v_part[0:1, 0], ALU.subtract))
            link(V.tensor_copy(v_part[0:1, 1], v_rest[0:1, 0]))
            link(V.tensor_tensor(v_rest[0:1, 1], v_rest[0:1, 0], v_part[0:1, 1], ALU.subtract))
            V.tensor_copy(v_part[0:1, 2], v_rest[0:1, 1]).then_inc(v_split, 1)

            dve.wait_ge(all_as_floats, 3)
            V.tensor_tensor(all_src[:], all_src[:], all_dst[:], ALU.is_equal)
            link(V.tensor_tensor(all_next[:], all_next[:], all_dst[:], ALU.subtract))
            link(V.tensor_scalar(all_dst[:], all_next[:], 0.0, None, ALU.is_gt))
            V.tensor_tensor_reduce(all_flag[:], all_src[:], all_dst[:], 1.0, 0.0, ALU.mult, ALU.add, faults[0:P8, 1:2])
            link(V.tensor_scalar(all_next[:], all_next[:], 0.0, None, ALU.is_lt))
            V.tensor_reduce(faults[0:P8, 0:1], all_next[:], mybir.AxisListType.X, ALU.add)
            link(V.tensor_scalar(faults[0:P8, 1:2], faults[0:P8, 1:2], float(N // P8), None, ALU.subtract))

            M = WIN - 1

            def pack(s):
                dve.wait_ge(win_as_floats, 2 * s + 2)
                link(V.tensor_tensor(win_a[:, s, 0:M], win_dst[:, s, 0:M], win_dst[:, s, 1:], ALU.is_equal))
                link(V.tensor_tensor(win_b[:, s, 0:M], win_dst[:, s, 0:M], win_src[:, s, 0:M], ALU.not_equal))
                link(V.tensor_tensor(win_a[:, s, 0:M], win_a[:, s, 0:M], win_b[:, s, 0:M], ALU.max))
                link(V.tensor_scalar(win_dst[:, s, 0:M], win_dst[:, s, 0:M], base_col[:, s:s + 1], None, ALU.subtract))

            def pack_rest(s):
                link(V.scalar_tensor_tensor(win_b[:, s, 0:M], win_dst[:, s, 0:M], 0.0, win_a[:, s, 0:M],
                                            ALU.is_ge, ALU.mult))
                link(V.scalar_tensor_tensor(win_a[:, s, 0:M], win_dst[:, s, 0:M], float(SUB), win_b[:, s, 0:M],
                                            ALU.is_lt, ALU.mult))
                V.scalar_tensor_tensor(win_dst_i[:, s, 0:M], win_dst[:, s, 0:M], 2049.0, win_a[:, s, 0:M],
                                       ALU.add, ALU.mult)
                link(V.tensor_tensor(win_src_i[:, s, 0:M], win_src[:, s, 0:M], win_a[:, s, 0:M], ALU.mult))
                V.scalar_tensor_tensor(packed[:, s, :], win_dst_i[:, s, 0:M], 17, win_src_i[:, s, 0:M],
                                       ALU.logical_shift_left, ALU.bitwise_or).then_inc(taken[s], 1)

            def take_max(s, r2):
                dve.wait_ge(taken[s], r2 + 1)
                dve.sem_inc(rounds_begun, 1)
                V.max(largest[:], packed[:, s, :].bitcast(F32)).then_inc(taken[s], 1)

            def take_out(s, r2):
                dve.wait_ge(taken[s], r2 + 2)
                V.tensor_copy(found[:, s, bass.ds(r2 * 4 + 1, 8)], largest[:])
                V.match_replace(packed[:, s, :].bitcast(F32), largest[:],
                                packed[:, s, :].bitcast(F32), 0.0).then_inc(taken[s], 1)

            def unpack(s):
                dve.wait_ge(taken[s], 2 * ROUNDS + 1)
                bits = found[:, s, 0:SLOTS].bitcast(I32)
                V.tensor_scalar(found_i[:, 0, s, :], bits, (1 << 17) - 1, None, ALU.bitwise_and)
                link(V.tensor_scalar(found_i[:, 1, s, :], bits, 17, 2047, ALU.logical_shift_right, ALU.bitwise_and))
                V.tensor_copy(found_f[:, 0, s, :], found_i[:, 0, s, :])
                link(V.tensor_scalar(found_f[:, 1, s, :], found_i[:, 1, s, :], 1.0, None, ALU.subtract))
                V.tensor_scalar(found_f[:, 2, s, :], found_f[:, 1, s, :], 0.0, base_col[:, s:s + 1],
                                ALU.max, ALU.add).then_inc(found_made, 1)
                last = V.tensor_reduce(faults[:, 2 + s:3 + s], packed[:, s, :].bitcast(F32), mybir.AxisListType.X, ALU.max)
                if s == SETS - 1:
                    link(last)
                    link(V.tensor_tensor(faults[:, 2:], faults[:, 2:], found[:, :, SLOTS], ALU.max))
                    V.tensor_scalar(faults[:, 2:], faults[:, 2:], 0.0, None, ALU.is_gt).then_inc(faults_counted, 1)

            def fill_tables(s):
                dve.wait_ge(found_turned, s + 1)
                first = SET_STEPS * s
                count = min(SET_STEPS, STEPS - first)
                for k, to in enumerate((edge_idx[:, first:first + count, 0:2],
                                        edge_loc[:, 2 * first:2 * (first + count)].rearrange("p (i h) -> p i h", h=2),
                                        edge_idx[:, first:first + count, 2:4])):
                    V.tensor_copy(to, ps_g[:, k * 128:k * 128 + 2 * count].rearrange("p (i h) -> p i h", h=2)
                                  ).then_inc(index_made, 1)
                if s == SETS - 1:
                    link(V.tensor_copy(faults_sum[:], ps_g[0:1, 384:386 + SETS]))
                    link(V.tensor_tensor(faults_sum[:], faults_sum[:], faults_sum[:], ALU.mult))
                    link(V.tensor_reduce(faults_all[:], faults_sum[:], mybir.AxisListType.X, ALU.max))
                    V.tensor_scalar(general_i[:], faults_all[:], 1.0, None, ALU.min).then_inc(path_chosen, 1)
                    dve.wait_ge(path_chosen, 1)
                dve.wait_ge(index_made, 3 * s + 3)

            pack(0)
            pack_rest(0)
            for r in range(ROUNDS):
                take_max(0, 2 * r)
                take_out(0, 2 * r)
            unpack(0)
            fill_tables(0)
            pack(1)
            pack_rest(1)

            for L in layers:
                n = L.n

                def place(i, slot):
                    if exists(i, 2):
                        dve.wait_ge(L["z1_ps"], i - 1)
                    V.tensor_copy(loc_now[:, slot, :], edge_loc[:, bass.ds(i * 2, 2)]).then_inc(L["loc_made"], 1)

                def turn(i, slot):
                    dve.wait_ge(L["xh_made"], i + 1)
                    V.tensor_tensor(x_part[:, slot, 1, :].rearrange("p (s c) -> p s c", s=HALVES), ps_x[:, :, 0:SUB],
                                    x_part[:, slot, 0, :].bitcast(F32).rearrange("p (s c) -> p s c", s=HALVES),
                                    ALU.subtract).then_inc(L["xl_made"], 1)

                def messages(i, slot):
                    def mark(h):
                        V.tensor_scalar(onehot[:, slot, h, :], node_iota[:].rearrange("p t q -> p (t q)"),
                                        loc_now[:, slot, h:h + 1], None, ALU.is_equal).then_inc(L["onehot_made"], 1)

                    dve.wait_ge(L["loc_made"], i + 1)
                    dve.wait_ge(L["mh_made"], i + 1)
                    V.tensor_tensor(msg_rest[:, slot, :], ps_e[:, 2 * C:4 * C], msg_part[:, slot, 0, :],
                                    ALU.subtract).then_inc(L["mrest_made"], 1)
                    mark(0)
                    dve.wait_ge(L["mrest_made"], i + 1)
                    V.tensor_copy(msg_part[:, slot, 1, :], msg_rest[:, slot, :]).then_inc(L["mmid_made"], 1)
                    mark(1)
                    dve.wait_ge(L["mmid_made"], i + 1)
                    V.tensor_tensor(msg_part[:, slot, 2, :], msg_rest[:, slot, :], msg_part[:, slot, 1, :],
                                    ALU.subtract).then_inc(L["mout_made"], 1)

                def square_sums(i, slot, s):
                    dve.wait_ge(L["z_read"][s], i + 1)
                    for t in range(s * TILES, (s + 1) * TILES):
                        last = V.tensor_tensor_reduce(squares[:, slot, t, :], z_relu[:, slot, t, :], z_relu[:, slot, t, :],
                                                      1.0, 0.0, ALU.mult, ALU.add, sumsq[:, slot, t:t + 1])
                    if s == 1:
                        last.then_inc(L["stats_made"], 1)

                def floor(i, slot):
                    dve.wait_ge(L["stats_made"], i + 1)
                    V.tensor_scalar(sumsq_min[:, slot, :], sumsq[:, slot, :], NORM_EPS ** 2, None,
                                    ALU.max).then_inc(L["sums_min"], 1)

                def residual(i, slot, s):
                    dve.wait_ge(L["z_ps"][s], i + 1)
                    if s == 0:
                        dve.wait_ge(L["res_loaded"][slot], slot_loads(i, slot))
                    if exists(i, 2):
                        dve.wait_ge(L["out_begun" if s == 0 else "out_made"], i - 1)
                    V.tensor_tensor(y_sum[:, slot, s * TILES:(s + 1) * TILES, :].rearrange("p t c -> p (t c)"),
                                    ps_z[0:PN, s, 0:TILES * C], res_in[:, slot, s, :], ALU.add).then_inc(L["z_read"][s], 1)
                    dve.wait_ge(L["z_read"][s], i + 1)
                    for t in range(s * TILES, (s + 1) * TILES):
                        last = V.bn_stats(stats[:, slot, t, :], y_sum[:, slot, t, :])
                    if s == 1:
                        last.then_inc(L["stats_made"], 1)

                def variances(i, slot):
                    dve.wait_ge(L["stats_made"], i + 1)
                    dve.sem_inc(L["sums_begun"], 1)
                    for t in range(HALVES * TILES):
                        last = V.bn_aggr(meanvar[:, slot, t, :], stats[:, slot, t, :])
                    last.then_inc(L["var_made"], 1)
                    dve.wait_ge(L["var_made"], i + 1)
                    V.tensor_scalar(sumsq_min[:, slot, :], meanvar[:, slot, :, 1], LN_EPS, None,
                                    ALU.add).then_inc(L["sums_min"], 1)

                def inverse_root(i, slot):
                    dve.wait_ge(L["root_made"], i + 1)
                    V.reciprocal(rinv[:, slot, :], root[:, slot, :]).then_inc(L["root_inverted"], 1)

                def normalise(i, slot):
                    if exists(i, 2):
                        dve.wait_ge(L["stored"][slot], slot_loads(i, slot) - 16)
                    dve.wait_ge(L["root_inverted"], i + 1)
                    V.tensor_tensor(y_out[:, slot, :, :], z_relu[:, slot, :, :],
                                    rinv[:, slot, :].unsqueeze(2).to_broadcast([PN, HALVES * TILES, C]),
                                    ALU.mult).then_inc(L["out_made"], 1)

                def shift_of(i, slot):
                    dve.wait_ge(L["root_inverted"], i + 1)
                    V.scalar_tensor_tensor(shift[:, slot, :], meanvar[:, slot, :, 0], -1.0, rinv[:, slot, :],
                                           ALU.mult, ALU.mult).then_inc(L["rinv_made"], 1)

                def step(i, slot, finding=None):
                    if exists(i, 1):
                        if n == 0:
                            square_sums(i - 1, 1 - slot, 1)
                            floor(i - 1, 1 - slot)
                        else:
                            residual(i - 1, 1 - slot, 1)
                    turn(i + 1, 1 - slot)
                    if n == 0:
                        if exists(i, 1):
                            inverse_root(i - 1, 1 - slot)
                        place(i + 1, 1 - slot)
                        if exists(i, 1):
                            normalise(i - 1, 1 - slot)
                        if finding and slot == 0:
                            take_max(finding, i - found_by(finding - 1))
                        if finding and slot == 1:
                            take_out(finding, i - 1 - found_by(finding - 1))
                        square_sums(i, slot, 0)
                        messages(i + 1, 1 - slot)
                    else:
                        if exists(i, 1):
                            variances(i - 1, 1 - slot)
                        residual(i, slot, 0)
                        if exists(i, 1):
                            inverse_root(i - 1, 1 - slot)
                        place(i + 1, 1 - slot)
                        if exists(i, 1):
                            shift_of(i - 1, 1 - slot)
                        messages(i + 1, 1 - slot)

                turn(0, 0)
                place(0, 0)
                if n == 0:
                    pack(2)
                messages(0, 0)
                if n == 0:
                    step(0, 0)
                    pack_rest(2)
                    step(1, 1)
                    first = 2
                    for s in range(1, SETS):
                        until = found_by(s)
                        over_steps(dve, lambda i, slot: step(i, slot, s), first, until)
                        unpack(s)
                        step(until, 0, s + 1 if s + 1 < SETS else None)
                        step(until + 1, 1, s + 1 if s + 1 < SETS else None)
                        fill_tables(s)
                        first = until + 2
                    over_steps(dve, step, first)
                else:
                    over_steps(dve, step, unrolled=4)
                if n == 0:
                    square_sums(LAST - 1, 1, 1)
                    floor(LAST - 1, 1)
                    inverse_root(LAST - 1, 1)
                    normalise(LAST - 1, 1)
                    square_sums(LAST, 0, 0)
                    square_sums(LAST, 0, 1)
                    floor(LAST, 0)
                    inverse_root(LAST, 0)
                    normalise(LAST, 0)
                else:
                    residual(LAST - 1, 1, 1)
                    residual(LAST, 0, 0)
                    variances(LAST - 1, 1)
                    inverse_root(LAST - 1, 1)
                    shift_of(LAST - 1, 1)
                    residual(LAST, 0, 1)
                    variances(LAST, 0)
                    inverse_root(LAST, 0)
                    shift_of(LAST, 0)

            with dve.If(takes_general_path(dve)):
                for G in general:
                    n = G.n
                    with dve.Fori(0, ERWS) as r:
                        at = [0]

                        def link_edge(ins):
                            at[0] += 1
                            ins.then_inc(G["g_dve"], 1)
                            dve.wait_ge(G["g_dve"], r * 7 + at[0])

                        dve.wait_ge(G["g_edges_loaded"], r * 48 + 48)
                        link_edge(V.tensor_copy(e_dst[:], e_dst_i[:]))
                        link_edge(V.tensor_copy(e_row[:], e_row_i[:]))
                        link_edge(V.tensor_scalar(e_same[:], e_row[:], e_dst[:, 0:1], None, ALU.is_equal))
                        link_edge(V.tensor_tensor(e_earlier[:], e_same[:], before[0:ROW, 0:ROW], ALU.mult))
                        link_edge(V.tensor_reduce(e_count[:], e_earlier[:], mybir.AxisListType.X, ALU.max))
                        link_edge(V.tensor_scalar(e_skip[:], e_count[:], float(N), None, ALU.mult))
                        link_edge(V.tensor_tensor(e_put_i[:], e_skip[:], e_dst[:], ALU.add))
                        dve.wait_ge(G["g_mout"], r + 1)
                        V.tensor_copy(e_out[:], ps_u[0:ROW, 0, 0:C]).then_inc(G["g_mout_made"], 1)
                        dve.wait_ge(G["g_sum"], r + 1)
                        dve.wait_ge(G["g_acc_gathered"], r * 16 + 16)
                        V.tensor_tensor(e_new[:], ps_z[0:ROW, 0, 0:C], e_acc[:], ALU.add).then_inc(G["g_sum_made"], 1)
                    T = HALVES * TILES
                    flat = "p s (t c) -> p (s t) c"
                    for i in over_nodes(dve):
                        at = [0]

                        def link_node(ins):
                            at[0] += 1
                            ins.then_inc(G["g_node_dve"], 1)
                            dve.wait_ge(G["g_node_dve"], i * (3 + n) + at[0])

                        dve.wait_ge(G["g_acc_loaded"], i * 32 + 32)
                        z = x_in[:, 0, :, :].rearrange(flat, t=TILES)
                        y = y_out[:, 0, :, :]
                        if n == 0:
                            link_node(V.tensor_scalar(z_relu[:, 0, :, :], z, 0.0, None, ALU.max))
                            for t in range(T):
                                last = V.tensor_tensor_reduce(squares[:, 0, t, :], z_relu[:, 0, t, :], z_relu[:, 0, t, :],
                                                              1.0, 0.0, ALU.mult, ALU.add, sumsq[:, 0, t:t + 1])
                            link_node(last)
                            V.tensor_scalar(sumsq_min[:, 0, :], sumsq[:, 0, :], NORM_EPS ** 2, None,
                                            ALU.max).then_inc(G["g_sums_made"], 1)
                        else:
                            link_node(V.tensor_tensor(z_relu[:, 0, :, :], z, res_in[:, 0, :, :].rearrange(flat, t=TILES),
                                                      ALU.add))
                            for t in range(T):
                                last = V.bn_stats(stats[:, 0, t, :], z_relu[:, 0, t, :])
                            link_node(last)
                            dve.sem_inc(G["g_begun"], 1)
                            for t in range(T):
                                last = V.bn_aggr(meanvar[:, 0, t, :], stats[:, 0, t, :])
                            link_node(last)
                            V.tensor_scalar(sumsq_min[:, 0, :], meanvar[:, 0, :, 1], LN_EPS, None,
                                            ALU.add).then_inc(G["g_sums_made"], 1)
                        dve.wait_ge(G["g_root_made"], i + 1)
                        link_node(V.reciprocal(rinv[:, 0, :], root[:, 0, :]))
                        for t in range(T):
                            if n == 0:
                                last = V.tensor_scalar(y[:, t, :], z_relu[:, 0, t, :], rinv[:, 0, t:t + 1], None, ALU.mult)
                            else:
                                last = V.tensor_scalar(y[:, t, :], z_relu[:, 0, t, :], meanvar[:, 0, t, 0:1],
                                                       rinv[:, 0, t:t + 1], ALU.subtract, ALU.mult)
                        last.then_inc(G["g_out_made"], 1)


_W = ("wa", "ba", "g", "be", "rm", "rv", "wb", "bb")
_NAMES = [{"wa": f"L0_gnn_w{n}a", "ba": f"L0_gnn_b{n}a", "g": f"L0_gnn_g{n}", "be": f"L0_gnn_be{n}",
           "rm": f"L0_gnn_rm{n}", "rv": f"L0_gnn_rv{n}", "wb": f"L0_gnn_w{n}b", "bb": f"L0_gnn_b{n}b"} for n in (1, 2)]
_INS = ["x", "src", "dst"] + [d[k] for d in _NAMES for k in _W]


def kernel(**inputs):
    import numpy as _np
    import concourse.bacc as _bacc
    from concourse import mybir as _mybir
    from concourse.bass_utils import run_bass_kernel_spmd as _run

    nc = _bacc.Bacc("TRN2", target_bir_lowering=False, num_devices=1)
    arrays, aps = {}, {}
    for name in _INS:
        a = _np.ascontiguousarray(inputs[name])
        arrays[f"in_{name}_dram"] = a
        aps[name] = nc.dram_tensor(f"in_{name}_dram", a.shape, _mybir.dt.from_np(a.dtype), kind="ExternalInput").ap()
    out = nc.dram_tensor("out_dram", inputs["x"].shape, _mybir.dt.float32, kind="ExternalOutput").ap()
    gnn_kernel(nc, aps["x"], aps["src"], aps["dst"], [{k: aps[d[k]] for k in _W} for d in _NAMES], out)
    r = _run(nc, [arrays], core_ids=[0])
    return r.results[0]["out_dram"]
```
